# Optimizing a Trainium2 kernel written in Bass

```python
import numpy as np
import jax
import jax.numpy as jnp

def _softmax(x, axis=-1):
    return jax.nn.softmax(x, axis=axis)

def _gelu(x):
    return jax.nn.gelu(x, approximate=True)

def _silu(x):
    return jax.nn.silu(x)

def _sigmoid(x):
    return jax.nn.sigmoid(x)

def _layernorm(x, axis=-1, eps=1e-05):
    m = jnp.mean(x, axis=axis, keepdims=True)
    v = jnp.var(x, axis=axis, keepdims=True)
    return (x - m) / jnp.sqrt(v + eps)

def _scatter_add(tgt, idx, src, axis=0):
    return tgt.at[idx].add(src)

def _segment_sum(src, seg, n):
    return jax.ops.segment_sum(src, seg, n)
kernel_name = 'mk_flamingo_gated_d1_seqx_r8_0db9f5'

def setup_inputs(seed: int=0):
    np.random.seed(seed)
    _w = jnp.asarray

    def _rec_inputs():
        import jax
        import jax.numpy as jnp
        _rk = jax.random.key(seed)
        x = -0.0005207 + 1.001 * jax.random.normal(jax.random.fold_in(_rk, 1), (32, 64, 512), jnp.float32)
        _lenS = 64 - jax.random.randint(jax.random.fold_in(_rk, 7), (32,), 0, max(1, 64 // 4) + 1, jnp.int32)
        _lenS2 = 64 - jax.random.randint(jax.random.fold_in(_rk, 8), (32,), 0, max(1, 64 // 4) + 1, jnp.int32)
        _ctx_4096P = jax.random.normal(jax.random.fold_in(_rk, 11), (32, 16, 512), jnp.float32)
        _ctx_4096c = jax.random.dirichlet(jax.random.fold_in(_rk, 511), 0.3 * jnp.ones((16,), jnp.float32), (32, 64))
        _ctx_4096t = jnp.einsum('bsk,bkd->bsd', _ctx_4096c, _ctx_4096P)
        _ctx_4096t = _ctx_4096t * jax.lax.rsqrt(jnp.mean(jnp.square(_ctx_4096t)) + 1e-12) * 0.953939
        ctx_4096 = -0.00010331 + 0.999899 * (_ctx_4096t + 0.3 * jax.random.normal(jax.random.fold_in(_rk, 611), (32, 64, 512), jnp.float32))
        _g = jax.random.normal(jax.random.fold_in(_rk, 9001), (2, 1), jnp.float32)
        _g = jnp.sign(_g) * jnp.maximum(jnp.abs(_g), 1.0) + (_g == 0) * 1.0
        g_xattn = _g[0]
        g_ffn = _g[1]
        return (x, ctx_4096, g_xattn, g_ffn)
    x, ctx_4096, g_xattn, g_ffn = _rec_inputs()

    def _L0_xattn_setup():
        import jax, jax.numpy as jnp
        import numpy as np
        import math
        HIDDEN = 512
        N_HEADS = 32
        HEAD_DIM = 128
        N_KV_HEADS = 4
        N_GROUPS = N_HEADS // N_KV_HEADS
        key = jax.random.key(seed)
        ks = jax.random.split(key, 6)
        B, NL, S = (8, 64, 512)
        latents = jax.random.normal(ks[0], (B, NL, HIDDEN), dtype=jnp.float32)
        context = jax.random.normal(ks[1], (B, S, HIDDEN), dtype=jnp.float32)
        scale = 1.0 / math.sqrt(HIDDEN)
        Wq = jax.random.normal(ks[2], (HIDDEN, N_HEADS * HEAD_DIM), dtype=jnp.float32) * scale
        Wk = jax.random.normal(ks[3], (HIDDEN, N_KV_HEADS * HEAD_DIM), dtype=jnp.float32) * scale
        Wv = jax.random.normal(ks[4], (HIDDEN, N_KV_HEADS * HEAD_DIM), dtype=jnp.float32) * scale
        Wo = jax.random.normal(ks[5], (N_HEADS * HEAD_DIM, HIDDEN), dtype=jnp.float32) * scale
        return {'latents': latents, 'context': context, 'Wq': Wq, 'Wk': Wk, 'Wv': Wv, 'Wo': Wo}
    _L0_xattn_all = _L0_xattn_setup()
    _L0_xattn_in = {k: v for k, v in _L0_xattn_all.items() if k in ('Wq', 'Wk', 'Wv', 'Wo')}
    del _L0_xattn_all

    def _L0_ffn_setup():
        import jax, jax.numpy as jnp
        import numpy as np
        DIM = 512
        INTER = 128
        E = 16
        GROUPS = 4
        LIM = 2
        K = 2
        SHARED_INTER = 2 * INTER
        SCALE = 1.0
        key = jax.random.key(seed)
        ks = jax.random.split(key, 16)

        def n(k, shape, s=0.02):
            return jax.random.normal(k, shape, jnp.float32) * s
        return {'x': jax.random.normal(ks[0], (1, 256, DIM), jnp.float32), 'router_w': n(ks[1], (DIM, E)), 'router_b': n(ks[2], (E,)), 'router_bias': n(ks[3], (E,), 1.0), 'ew1': n(ks[4], (E, DIM, INTER)), 'eb1': n(ks[5], (E, INTER)), 'ew2': n(ks[6], (E, DIM, INTER)), 'eb2': n(ks[7], (E, INTER)), 'ew3': n(ks[8], (E, INTER, DIM)), 'eb3': n(ks[9], (E, DIM)), 'sw1': n(ks[10], (DIM, SHARED_INTER)), 'sb1': n(ks[11], (SHARED_INTER,)), 'sw2': n(ks[12], (DIM, SHARED_INTER)), 'sb2': n(ks[13], (SHARED_INTER,)), 'sw3': n(ks[14], (SHARED_INTER, DIM)), 'sb3': n(ks[15], (DIM,))}
    _L0_ffn_all = _L0_ffn_setup()
    _L0_ffn_in = {k: v for k, v in _L0_ffn_all.items() if k in ('router_w', 'router_b', 'router_bias', 'ew1', 'eb1', 'ew2', 'eb2', 'ew3', 'eb3', 'sw1', 'sb1', 'sw2', 'sb2', 'sw3', 'sb3')}
    del _L0_ffn_all
    return {'x': x, 'ctx_4096': ctx_4096, 'g_xattn': g_xattn, 'g_ffn': g_ffn, 'L0_xattn_Wq': _L0_xattn_in['Wq'], 'L0_xattn_Wk': _L0_xattn_in['Wk'], 'L0_xattn_Wv': _L0_xattn_in['Wv'], 'L0_xattn_Wo': _L0_xattn_in['Wo'], 'L0_ffn_router_w': _L0_ffn_in['router_w'], 'L0_ffn_router_b': _L0_ffn_in['router_b'], 'L0_ffn_router_bias': _L0_ffn_in['router_bias'], 'L0_ffn_ew1': _L0_ffn_in['ew1'], 'L0_ffn_eb1': _L0_ffn_in['eb1'], 'L0_ffn_ew2': _L0_ffn_in['ew2'], 'L0_ffn_eb2': _L0_ffn_in['eb2'], 'L0_ffn_ew3': _L0_ffn_in['ew3'], 'L0_ffn_eb3': _L0_ffn_in['eb3'], 'L0_ffn_sw1': _L0_ffn_in['sw1'], 'L0_ffn_sb1': _L0_ffn_in['sb1'], 'L0_ffn_sw2': _L0_ffn_in['sw2'], 'L0_ffn_sb2': _L0_ffn_in['sb2'], 'L0_ffn_sw3': _L0_ffn_in['sw3'], 'L0_ffn_sb3': _L0_ffn_in['sb3']}

def reference(x, ctx_4096, g_xattn, g_ffn, L0_xattn_Wq, L0_xattn_Wk, L0_xattn_Wv, L0_xattn_Wo, L0_ffn_router_w, L0_ffn_router_b, L0_ffn_router_bias, L0_ffn_ew1, L0_ffn_eb1, L0_ffn_ew2, L0_ffn_eb2, L0_ffn_ew3, L0_ffn_eb3, L0_ffn_sw1, L0_ffn_sb1, L0_ffn_sw2, L0_ffn_sb2, L0_ffn_sw3, L0_ffn_sb3):
    import jax
    import jax.numpy as jnp

    def _L0_xattn_ref(latents, context, Wq, Wk, Wv, Wo):
        import jax, jax.numpy as jnp
        import numpy as np
        import math
        HIDDEN = 512
        N_HEADS = 32
        HEAD_DIM = 128
        N_KV_HEADS = 4
        N_GROUPS = N_HEADS // N_KV_HEADS
        b, q_len, _ = latents.shape
        kv_len = q_len + context.shape[1]
        hidden_states = jnp.concatenate([context, latents], axis=1)
        q = (latents @ Wq).reshape(b, q_len, N_KV_HEADS, N_GROUPS, HEAD_DIM)
        k = (hidden_states @ Wk).reshape(b, kv_len, N_KV_HEADS, HEAD_DIM)
        v = (hidden_states @ Wv).reshape(b, kv_len, N_KV_HEADS, HEAD_DIM)
        scale = 1.0 / math.sqrt(HEAD_DIM)
        scores = jnp.einsum('bqhgd,bkhd->bhgqk', q, k) * scale
        attn = jax.nn.softmax(scores.astype(jnp.float32), axis=-1).astype(q.dtype)
        out = jnp.einsum('bhgqk,bkhd->bqhgd', attn, v)
        out = out.reshape(b, q_len, N_HEADS * HEAD_DIM)
        return out @ Wo

    def _L0_ffn_ref(x, router_w, router_b, router_bias, ew1, eb1, ew2, eb2, ew3, eb3, sw1, sb1, sw2, sb2, sw3, sb3):
        import jax, jax.numpy as jnp
        import numpy as np
        DIM = 512
        INTER = 128
        E = 16
        GROUPS = 4
        LIM = 2
        K = 2
        SHARED_INTER = 2 * INTER
        SCALE = 1.0
        shape = x.shape
        xt = x.reshape(-1, DIM)
        T = xt.shape[0]
        logits = xt @ router_w + router_b
        scores = jax.nn.softmax(logits.astype(jnp.float32), axis=-1) + router_bias
        g = scores.reshape(T, GROUPS, E // GROUPS)
        _, gidx = jax.lax.top_k(g.max(axis=-1), LIM)
        keep = jnp.zeros((T, GROUPS), bool).at[jnp.arange(T)[:, None], gidx].set(True)
        masked = jnp.where(keep[:, :, None], g, -jnp.inf).reshape(T, E)
        _, idx = jax.lax.top_k(masked, K)
        vals = (jnp.take_along_axis(scores, idx, axis=1) * SCALE).astype(x.dtype)
        gate = jnp.zeros((T, E), x.dtype).at[jnp.arange(T)[:, None], idx].add(vals)

        def step(y, p):
            w1, b1, w2, b2, w3, b3, ge = p
            h = jax.nn.silu(xt @ w1 + b1) * (xt @ w2 + b2)
            return (y + ge[:, None] * (h @ w3 + b3), None)
        y, _ = jax.lax.scan(step, jnp.zeros_like(xt), (ew1, eb1, ew2, eb2, ew3, eb3, gate.T))
        z = jax.nn.silu(xt @ sw1 + sb1) * (xt @ sw2 + sb2) @ sw3 + sb3
        return (y + z).reshape(shape)
    x = x + jnp.tanh(g_xattn[0]) * _L0_xattn_ref(_layernorm(x, axis=-1), ctx_4096, L0_xattn_Wq, L0_xattn_Wk, L0_xattn_Wv, L0_xattn_Wo)
    x = x + jnp.tanh(g_ffn[0]) * _L0_ffn_ref(_layernorm(x, axis=-1), L0_ffn_router_w, L0_ffn_router_b, L0_ffn_router_bias, L0_ffn_ew1, L0_ffn_eb1, L0_ffn_ew2, L0_ffn_eb2, L0_ffn_ew3, L0_ffn_eb3, L0_ffn_sw1, L0_ffn_sb1, L0_ffn_sw2, L0_ffn_sb2, L0_ffn_sw3, L0_ffn_sb3)
    return x

_drawn_inputs = setup_inputs


def setup_inputs(seed=0):
    import zlib

    import numpy as np

    out = dict(_drawn_inputs(seed))
    spreads = {}
    factors = {'L0_ffn_router_w': 8.0,
     'L0_ffn_router_b': 64.0,
     'L0_ffn_eb1': 8.0,
     'L0_ffn_eb2': 8.0,
     'L0_ffn_sb1': 42.677,
     'L0_ffn_sb2': 41.825,
     'L0_ffn_sb3': 3.61}
    for name, (base, spread) in spreads.items():
        noise = np.random.default_rng([zlib.crc32(name.encode()), seed]).standard_normal(out[name].shape)
        drawn = base * np.exp(spread * noise) if base else spread * noise
        out[name] = jnp.asarray(drawn.astype(out[name].dtype))
    for name, factor in factors.items():
        out[name] = (out[name] * factor).astype(out[name].dtype)
    return out
```

```python
from contextlib import ExitStack

import numpy as np
import concourse.bass as bass
import concourse.mybir as mybir
from concourse.alu_op_type import AluOpType as ALU

ACT = mybir.ActivationFunctionType
AX = mybir.AxisListType
F32 = mybir.dt.float32
F32R = mybir.dt.float32r

P = 128
BATCH = 32
SQ = 64
SC = 64
D = 512
C = D // P
DH = 128
NKV = 4
HG = 8
T = BATCH * SQ
TILES = T // P
OCTETS = T // 512
QUADS = T // 256
QB = 4
KEYS = SQ + SC
E = 16
GROUPS = 4
INTER = 128
EPS = 1e-5
SCALE = DH ** -0.5
LOWEST = -3.0e38


class Buffers:

    def __init__(self, nc, stack):
        self.nc, self.stack = nc, stack

    def sb(self, name, shape, dt=F32):
        return self.stack.enter_context(self.nc.sbuf_tensor(name, shape, dt))

    def ps(self, name, shape, dt=F32):
        return self.stack.enter_context(self.nc.psum_tensor(name, shape, dt))

    def sem(self, name):
        return self.stack.enter_context(self.nc.semaphore(name))


def f32(ap):
    return ap.bitcast(F32)


def first(i):
    return isinstance(i, int) and i == 0


def three_pass(pe, out, w_hi, w_lo, x_hi, x_lo, first, last):
    pe.matmul(out, w_hi, x_hi, start=first, stop=False)
    pe.matmul(out, w_lo, x_hi, start=False, stop=False)
    return pe.matmul(out, w_hi, x_lo, start=False, stop=last)



def stage_one(nc, a, common, scratch):
    y, ident, ones_r = common["y"], common["ident"], common["ones_r"]
    gain_attn, gain_ffn = common["gain_attn"], common["gain_ffn"]
    with ExitStack() as stack:
        b = Buffers(nc, stack)
        ctx_raw = b.sb("ctx_raw", [P, 4, D])
        kv_raw = b.sb("kv_raw", [P, 2, C, D])
        wk_hi = b.sb("wk_hi", [P, C, D], F32R)
        wk_lo = b.sb("wk_lo", [P, C, D], F32R)
        wv_hi = b.sb("wv_hi", [P, C, D], F32R)
        wv_lo = b.sb("wv_lo", [P, C, D], F32R)
        tok_hi = b.sb("tok_hi", [P, 2, C, 512], F32R)
        tok_lo = b.sb("tok_lo", [P, 2, C, 512], F32R)
        k_out = [b.sb(f"k_out{i}", [P, 2, 2, QB, KEYS], F32R) for i in range(2)]
        v_out = [b.sb(f"v_out{i}", [P, NKV, 2, DH], F32R) for i in range(2)]
        normed = [b.sb(f"normed{i}", [P, D]) for i in range(2)]
        stats = b.sb("stats", [P, TILES, 6])
        mean_var = b.sb("mean_var", [P, TILES, 2])
        std = b.sb("std", [P, TILES])
        rstd = b.sb("rstd", [P, TILES])
        gates = b.sb("gates", [P, 2])
        eps = b.sb("eps", [P, 1])
        ones = b.sb("ones", [P, P])
        ps_t = [b.ps(f"ps_t{i}", [P, C, P]) for i in range(2)]
        ps_a = [b.ps(f"ps_a{i}", [P, 512]) for i in range(2)]

        x_in = b.sem("x_in")
        ctx_in = b.sem("ctx_in")
        kv_in = b.sem("kv_in")
        gates_in = b.sem("gates_in")
        consts_made = b.sem("consts_made")
        ones_copied = b.sem("ones_copied")
        gains_made = b.sem("gains_made")
        stats_made = b.sem("stats_made")
        meanvar_made = b.sem("meanvar_made")
        std_made = b.sem("std_made")
        rstd_made = b.sem("rstd_made")
        normed_made = b.sem("normed_made")
        kv_hi_made = b.sem("kv_hi_made")
        kv_lo_made = b.sem("kv_lo_made")
        transposed = b.sem("transposed")
        tok_hi_made = b.sem("tok_hi_made")
        tok_lo_made = b.sem("tok_lo_made")
        projected = b.sem("projected")
        out_hi_made = b.sem("out_hi_made")
        out_lo_made = b.sem("out_lo_made")
        k_stored = [b.sem(f"k_stored{i}") for i in range(2)]
        v_stored = [b.sem(f"v_stored{i}") for i in range(2)]
        x_stored = b.sem("x_stored")

        x_v = a["x"].rearrange("b s d -> (b s) d").rearrange("(o i p) d -> o p i d", i=4, p=P)
        ctx_v = a["ctx_4096"].rearrange("b s d -> (b s) d").rearrange("(o i p) d -> o p i d", i=4, p=P)
        UNITS = 8
        JOBS = 16

        block = stack.enter_context(nc.Block())

        @block.sync
        def _(sp):
            sp.dma_start(ctx_raw[:], ctx_v[0]).then_inc(ctx_in, 16)
            sp.dma_start(y[:, 0:4, :], x_v[0]).then_inc(x_in, 16)
            sp.dma_start(kv_raw[:, 0], a["L0_xattn_Wv"].rearrange("(c p) n -> p c n", p=P)).then_inc(kv_in, 16)
            sp.wait_ge(kv_in, 16)
            sp.dma_start(kv_raw[:, 1], a["L0_xattn_Wk"].rearrange("(c p) n -> p c n", p=P)).then_inc(kv_in, 16)
            for o in range(1, OCTETS):
                sp.wait_ge(x_in, 16 * o)
                sp.dma_start(y[:, 4 * o:4 * o + 4, :], x_v[o]).then_inc(x_in, 16)

            def octet(o, more):
                for u in range(UNITS):
                    src, i = u % 2, u // 2
                    if u == 7:
                        if more:
                            sp.wait_ge(transposed, UNITS * o + 7)
                            sp.dma_start(ctx_raw[:], ctx_v[o + 1]).then_inc(ctx_in, 16)
                    sp.wait_ge(out_lo_made, JOBS * o + u + 1)
                    for bb in range(2):
                        batch = (i % 2) * 2 + bb
                        dst = scratch["v"][:, 2 * o + i // 2, src * 64:src * 64 + 64, batch]
                        sp.dma_start(dst.rearrange("g t h d -> t g (h d)"),
                                     f32(v_out[u % 2][64 * bb:64 * bb + 64]).rearrange("t g h d -> t g (h d)")
                                     ).then_inc(v_stored[u % 2], 16)
                for half in range(2):
                    for s, tok in enumerate((tok_hi, tok_lo)):
                        sp.dma_start(scratch["x"][2 * o + half, :, s],
                                     f32(tok[:, 1, :, 256 * half:256 * half + 256])).then_inc(x_stored, 16)
                for g in range(NKV):
                    sp.wait_ge(out_lo_made, JOBS * o + UNITS + 2 * g + 2)
                    sp.dma_start(scratch["k"][g, bass.ds(2 * o, 2)].rearrange("q p n -> p q n"),
                                 f32(k_out[g % 2][:]).rearrange("p q h b k -> p q (h b k)")
                                 ).then_inc(k_stored[g % 2], 16)

            with sp.Fori(0, OCTETS - 1) as o:
                octet(o, True)
            octet(OCTETS - 1, False)
            for i in range(2):
                sp.wait_ge(k_stored[i], 16 * OCTETS * NKV // 2)
                sp.wait_ge(v_stored[i], 16 * OCTETS * UNITS)
            sp.wait_ge(x_stored, 16 * 4 * OCTETS)

        @block.gpsimd
        def _(pool):
            pool.memset(ident[:], 0.0).then_inc(consts_made, 1)
            pool.memset(ones[:], 1.0).then_inc(consts_made, 1)
            pool.memset(eps[:], EPS).then_inc(consts_made, 1)
            pool.wait_ge(consts_made, 3)
            pool.affine_select(out=ident[:], in_=ident[:], compare_op=ALU.not_equal, fill=1.0, base=0,
                               pattern=[[-1, P]], channel_multiplier=1).then_inc(consts_made, 1)
            for i, name in enumerate(("g_xattn", "g_ffn")):
                src = a[name].rearrange("(a b) -> a b", a=1).to_broadcast([P, 1])
                pool.dma_start(gates[:, i:i + 1], src).then_inc(gates_in, 16)

        @block.scalar
        def _(act):
            def std_of(lo, hi):
                act.wait_ge(meanvar_made, hi)
                act.activation(std[:, lo:hi], mean_var[:, lo:hi, 1], ACT.Sqrt, bias=eps[:]).then_inc(std_made, 1)

            act.wait_ge(consts_made, 4)
            act.wait_ge(gates_in, 32)
            act.activation(gain_attn[:], gates[:, 0:1], ACT.Tanh).then_inc(gains_made, 1)
            act.activation(gain_ffn[:], gates[:, 1:2], ACT.Tanh).then_inc(gains_made, 1)
            act.activation(ones_r[:], ones[:], ACT.Copy).then_inc(ones_copied, 1)
            std_of(0, 4)
            for i, hi in enumerate((wv_hi, wk_hi)):
                act.wait_ge(kv_in, 16 * (i + 1))
                act.activation(hi[:], kv_raw[:, i], ACT.Copy).then_inc(kv_hi_made, 1)

            def octet(o):
                def tok(u):
                    src, i = u % 2, u // 2
                    act.wait_ge(transposed, UNITS * o + u + 1)
                    if u == 0 and not first(o):
                        act.wait_ge(x_stored, 64 * o)
                    act.activation(tok_hi[:, src, :, i * P:(i + 1) * P], ps_t[u % 2][:],
                                   ACT.Copy).then_inc(tok_hi_made, 1)

                def v_job(u):
                    act.wait_ge(projected, JOBS * o + u + 1)
                    if not (first(o) and u < 2):
                        act.wait_ge(v_stored[u % 2], 32 * (4 * o + u // 2))
                    act.activation(v_out[u % 2][:, :, 0, :], ps_a[u % 2][:].rearrange("p (g d) -> p g d", g=NKV),
                                   ACT.Copy).then_inc(out_hi_made, 1)

                tok(0)
                for u in range(1, UNITS):
                    tok(u)
                    v_job(u - 1)
                v_job(UNITS - 1)
                if first(o):
                    std_of(4, TILES)
                for g in range(NKV):
                    for src in range(2):
                        job = UNITS + 2 * g + src
                        act.wait_ge(projected, JOBS * o + job + 1)
                        if src == 0 and not (first(o) and g < 2):
                            act.wait_ge(k_stored[g % 2], 16 * (2 * o + g // 2))
                        act.activation(k_out[g % 2][:, :, 0, :, 64 * src:64 * src + 64],
                                       ps_a[job % 2][:].rearrange("p (q b t) -> p q b t", q=2, b=QB),
                                       ACT.Copy).then_inc(out_hi_made, 1)

            octet(0)
            with act.Fori(1, OCTETS) as o:
                octet(o)

        @block.vector
        def _(dve):
            def stats_of(lo, hi):
                for n in range(lo, hi):
                    dve.bn_stats(stats[:, n, :], y[:, n, :]).then_inc(stats_made, 1)
                for n in range(lo, hi):
                    dve.wait_ge(stats_made, n + 1)
                    dve.bn_aggr(mean_var[:, n, :], stats[:, n, :]).then_inc(meanvar_made, 1)

            def rstd_of(lo, hi, count):
                dve.wait_ge(std_made, count)
                dve.reciprocal(rstd[:, lo:hi], std[:, lo:hi]).then_inc(rstd_made, 1)

            dve.wait_ge(x_in, 16)
            stats_of(0, 4)
            rstd_of(0, 4, 1)
            dve.wait_ge(rstd_made, 1)

            def normalise(o, i):
                if not (first(o) and i < 2):
                    dve.wait_ge(transposed, UNITS * o + 2 * i - 2)
                n = 4 * o + i
                n = slice(n, n + 1) if first(o) else bass.ds(n, 1)
                dve.tensor_scalar(normed[i % 2][:], y[:, n, :].squeeze(1), mean_var[:, n, 0],
                                  rstd[:, n], ALU.subtract, ALU.mult).then_inc(normed_made, 1)

            def octet(o):
                def tok_low(u):
                    src, i = u % 2, u // 2
                    dve.wait_ge(tok_hi_made, UNITS * o + u + 1)
                    dve.tensor_tensor(tok_lo[:, src, :, i * P:(i + 1) * P], ps_t[u % 2][:],
                                      f32(tok_hi[:, src, :, i * P:(i + 1) * P]),
                                      ALU.subtract).then_inc(tok_lo_made, 1)

                def v_low(u):
                    dve.wait_ge(out_hi_made, JOBS * o + u + 1)
                    dve.tensor_tensor(v_out[u % 2][:, :, 1, :], ps_a[u % 2][:].rearrange("p (g d) -> p g d", g=NKV),
                                      f32(v_out[u % 2][:, :, 0, :]), ALU.subtract).then_inc(out_lo_made, 1)

                normalise(o, 0)
                normalise(o, 1)
                tok_low(0)
                if first(o):
                    dve.wait_ge(kv_hi_made, 1)
                    dve.tensor_tensor(wv_lo[:], kv_raw[:, 0], f32(wv_hi[:]), ALU.subtract).then_inc(kv_lo_made, 1)
                for u in range(1, UNITS):
                    tok_low(u)
                    if u in (1, 3):
                        normalise(o, 2 + u // 2)
                    v_low(u - 1)
                    if first(o) and u < 7:
                        if u % 2:
                            dve.wait_ge(x_in, 16 * (u // 2 + 2))
                        stats_of(2 + 2 * u, 4 + 2 * u)
                v_low(UNITS - 1)
                if first(o):
                    dve.wait_ge(kv_hi_made, 2)
                    dve.tensor_tensor(wk_lo[:], kv_raw[:, 1], f32(wk_hi[:]), ALU.subtract).then_inc(kv_lo_made, 1)
                if first(o):
                    rstd_of(4, TILES, 2)
                    dve.wait_ge(rstd_made, 2)
                for g in range(NKV):
                    for src in range(2):
                        job = UNITS + 2 * g + src
                        keys = slice(64 * src, 64 * src + 64)
                        dve.wait_ge(out_hi_made, JOBS * o + job + 1)
                        for q in range(2):
                            last = dve.tensor_tensor(
                                k_out[g % 2][:, q, 1, :, keys],
                                ps_a[job % 2][:, 256 * q:256 * q + 256].rearrange("p (b t) -> p b t", b=QB),
                                f32(k_out[g % 2][:, q, 0, :, keys]), ALU.subtract)
                        last.then_inc(out_lo_made, 1)

            octet(0)
            with dve.Fori(1, OCTETS) as o:
                octet(o)

        @block.tensor
        def _(pe):
            pe.wait_ge(consts_made, 4)

            def octet(o):

                def transposes(u):
                    src, i = u % 2, u // 2
                    if u == 0:
                        pe.wait_ge(ctx_in, 16 * (o + 1))
                    if src == 1:
                        pe.wait_ge(normed_made, 4 * o + i + 1)
                    if not (first(o) and u < 2):
                        pe.wait_ge(tok_lo_made, UNITS * o + u - 1)
                    tile = normed[i % 2] if src else ctx_raw[:, i, :]
                    for c in range(C):
                        last = pe.transpose(ps_t[u % 2][:, c, :], tile[:, c * P:(c + 1) * P], ident[:])
                    last.then_inc(transposed, 1)

                def free_ps_a(job):
                    if not (first(o) and job < 2):
                        pe.wait_ge(out_lo_made, JOBS * o + job - 1)

                def v_job(u):
                    src, i = u % 2, u // 2
                    if first(o) and u == 0:
                        pe.wait_ge(kv_lo_made, 1)
                    pe.wait_ge(tok_lo_made, UNITS * o + u + 1)
                    free_ps_a(u)
                    for c in range(C):
                        t = slice(i * P, (i + 1) * P)
                        last = three_pass(pe, ps_a[u % 2][:], tok_hi[:, src, c, t], tok_lo[:, src, c, t],
                                          wv_hi[:, c, :], wv_lo[:, c, :], c == 0, c == C - 1)
                    last.then_inc(projected, 1)

                transposes(0)
                for u in range(1, UNITS):
                    transposes(u)
                    v_job(u - 1)
                v_job(UNITS - 1)
                if first(o):
                    pe.wait_ge(kv_lo_made, 2)
                for g in range(NKV):
                    for src in range(2):
                        job = UNITS + 2 * g + src
                        free_ps_a(job)
                        for c in range(C):
                            n = slice(g * DH, (g + 1) * DH)
                            last = three_pass(pe, ps_a[job % 2][:], wk_hi[:, c, n], wk_lo[:, c, n],
                                              tok_hi[:, src, c, :], tok_lo[:, src, c, :], c == 0, c == C - 1)
                        last.then_inc(projected, 1)

            octet(0)
            with pe.Fori(1, OCTETS) as o:
                octet(o)



def over_octets(eng, octet):
    octet(0, 0, 0)
    with eng.Fori(1, 3) as t:
        octet(t, t, 0)
    with eng.Fori(1, NKV) as g:
        octet(4 * g - 1, 3, g)
        octet(4 * g, 0, g)
        with eng.Fori(1, 3) as o:
            octet(4 * g + o, o, g)
    octet(15, 3, NKV)


STEPS = NKV * BATCH


class Step:

    def __init__(self, t, j):
        self.t, self.j = t, j
        self.m = 8 * t + j
        plain = isinstance(t, int)
        self.pv = not plain or 2 <= self.m < STEPS + 2
        self.exp = not plain or 1 <= self.m < STEPS + 1
        self.scores = not plain or self.m < STEPS
        self.quad = 2 * t + 1 + j // 4
        self.query = not plain or self.quad < STEPS // 4
        self.out = not plain or 4 <= self.m < STEPS + 4
        self.pair = 4 * t - 2 + j // 2
        self.add = j % 2 == 0 and (not plain or self.m >= 6)
        self.pair_parity = (j // 2) % 2

    def at_least(self, m):
        return not isinstance(self.t, int) or self.m >= m


def stage_two(nc, a, common, scratch):
    y, ones_r, gain = common["y"], common["ones_r"], common["gain_attn"]
    with ExitStack() as stack:
        b = Buffers(nc, stack)
        wq_hi = b.sb("wq_hi", [P, C, HG * DH], F32R)
        wq_lo = b.sb("wq_lo", [P, C, HG * DH], F32R)
        wo_hi = b.sb("wo_hi", [P, HG, D], F32R)
        wo_lo = b.sb("wo_lo", [P, HG, D], F32R)
        w_raw = [b.sb(f"w_raw{i}", [P, 1024]) for i in range(2)]
        xt = [b.sb(f"xt{i}", [P, 2, C, 256], F32R) for i in range(2)]
        kt = [b.sb(f"kt{i}", [P, 2, QB, KEYS], F32R) for i in range(2)]
        vt = [b.sb(f"vt{i}", [KEYS, QB, 2, DH], F32R) for i in range(2)]
        q_hi = [b.sb(f"q_hi{i}", [P, HG, 256], F32R) for i in range(2)]
        q_lo = [b.sb(f"q_lo{i}", [P, HG, 256], F32R) for i in range(2)]
        s_sb = [b.sb(f"s_sb{i}", [KEYS, 512]) for i in range(2)]
        s_max = [b.sb(f"s_max{i}", [KEYS, 512]) for i in range(2)]
        p_hi = [b.sb(f"p_hi{i}", [KEYS, 512], F32R) for i in range(2)]
        p_lo = [b.sb(f"p_lo{i}", [KEYS, 512], F32R) for i in range(2)]
        ones_col = b.sb("ones_col", [P, 1])
        turn = b.sb("turn", [P, 1])
        sums = b.sb("sums", [P, 16])
        rsums = b.sb("rsums", [P, 16])
        rsum_rows = b.sb("rsum_rows", [P, 512])
        o_sb = b.sb("o_sb", [P, HG, SQ])
        o_hi = [b.sb(f"o_hi{i}", [P, HG, P], F32R) for i in range(2)]
        o_lo = [b.sb(f"o_lo{i}", [P, HG, P], F32R) for i in range(2)]
        ps_q = [b.ps(f"ps_q{i}", [P, 512]) for i in range(2)]
        ps_s = [b.ps(f"ps_s{i}", [KEYS, 512]) for i in range(2)]
        ps_sum = b.ps("ps_sum", [P, 512])
        ps_o = [b.ps(f"ps_o{i}", [P, 512]) for i in range(2)]
        ps_y = b.ps("ps_y", [P, 512])

        raw_in = [b.sem(f"raw_in{i}") for i in range(2)]
        xt_in = [b.sem(f"xt_in{i}") for i in range(2)]
        kt_in = [b.sem(f"kt_in{i}") for i in range(2)]
        vt_in = [b.sem(f"vt_in{i}") for i in range(2)]
        col_made = b.sem("col_made")
        w_hi_made = b.sem("w_hi_made")
        w_lo_made = b.sem("w_lo_made")
        queries = b.sem("queries")
        q_hi_made = b.sem("q_hi_made")
        q_lo_made = b.sem("q_lo_made")
        scored = b.sem("scored")
        scores_copied = b.sem("scores_copied")
        max_made = b.sem("max_made")
        shifted = b.sem("shifted")
        exp_made = b.sem("exp_made")
        p_lo_made = b.sem("p_lo_made")
        summed = b.sem("summed")
        sums_read = b.sem("sums_read")
        rsums_made = b.sem("rsums_made")
        rsum_rows_made = b.sem("rsum_rows_made")
        weighted = b.sem("weighted")
        o_made = b.sem("o_made")
        o_hi_made = b.sem("o_hi_made")
        o_lo_made = b.sem("o_lo_made")
        halves = b.sem("halves")
        added = b.sem("added")

        wq_v = a["L0_xattn_Wq"].rearrange("(c p) (g n) -> g p c n", p=P, g=NKV)
        wo_v = a["L0_xattn_Wo"].rearrange("(g h d) n -> g d h n", g=NKV, h=HG)
        PIECES = 8

        def piece_raw(i):
            shape = dict(c=C) if i < 4 else dict(c=2)
            return w_raw[i % 2][:].rearrange("p (c n) -> p c n", **shape)

        def piece_of(w_q, w_o, i):
            return w_q[:, :, 256 * i:256 * i + 256] if i < 4 else w_o[:, 2 * i - 8:2 * i - 6, :]

        def splits_at(o, j):
            if isinstance(o, int) and o == 3 and 1 <= j <= 4:
                return [j - 1]
            if isinstance(o, int) and o == 0 and j in (3, 4):
                return [4, 5] if j == 3 else [6, 7]
            return []

        block = stack.enter_context(nc.Block())

        @block.sync
        def _(sp):
            def load_piece(g, i):
                if not (first(g) and i < 2):
                    sp.wait_ge(w_lo_made, PIECES * g + i - 1)
                src = wq_v[g, :, :, 256 * i:256 * i + 256] if i < 4 else wo_v[g, :, 2 * i - 8:2 * i - 6, :]
                sp.dma_start(piece_raw(i), src).then_inc(raw_in[i % 2], 16)

            def load_xt(quad_in_head, parity):
                sp.dma_start(f32(xt[parity][:]), scratch["x"][quad_in_head]).then_inc(xt_in[parity], 16)

            def load_kt(g, quad_in_head, parity):
                sp.dma_start(f32(kt[parity][:]).rearrange("p h b k -> p (h b k)"),
                             scratch["k"][g, quad_in_head]).then_inc(kt_in[parity], 16)

            def load_vt(g, quad_in_head, parity):
                sp.dma_start(f32(vt[parity][:]), scratch["v"][g, quad_in_head]).then_inc(vt_in[parity], 16)

            load_xt(0, 0)
            for i in range(PIECES):
                load_piece(0, i)
                if i == 4:
                    load_xt(1, 1)
                    load_kt(0, 0, 0)
                    load_vt(0, 0, 0)

            def octet(t, o, g):
                for half in range(2):
                    q = 2 * t + half
                    if isinstance(t, int) and q == QUADS * NKV - 1:
                        break
                    wraps = isinstance(o, int) and o == 3 and half == 1
                    next_quad = 0 if wraps else 2 * o + half + 1
                    head = g - 1 if isinstance(o, int) and o == 3 and not wraps else g
                    after = (2 * o + half + 2) % 8 if isinstance(o, int) else 2 * o + half + 2
                    if not (isinstance(t, int) and q + 2 >= QUADS * NKV):
                        sp.wait_ge(queries, 4 * q + 4)
                        load_xt(after, half)
                    if not first(q):
                        sp.wait_ge(scored, 4 * q)
                    load_kt(head, next_quad, 1 - half)
                    if not first(q):
                        sp.wait_ge(weighted, 4 * q)
                    load_vt(head, next_quad, 1 - half)
                    if half == 0 and isinstance(o, int) and o == 3 and not isinstance(t, int):
                        for i in range(4):
                            load_piece(g, i)
                    if half == 1 and isinstance(o, int) and o == 3 and not isinstance(t, int):
                        load_piece(g, 4)
                        load_piece(g, 5)
                    if half == 0 and isinstance(o, int) and o == 0 and not isinstance(t, int):
                        load_piece(g, 6)
                        load_piece(g, 7)

            over_octets(sp, octet)

        @block.gpsimd
        def _(pool):
            def step(m, parity):
                pool.wait_ge(scores_copied, m + 1)
                if not (isinstance(m, int) and m < 2):
                    pool.wait_ge(shifted, m - 1)
                    pool.tensor_tensor(turn[:], ones_col[:], ones_col[:], ALU.add)
                pool.partition_all_reduce(s_max[parity][:], s_sb[parity][:], KEYS,
                                          bass.bass_isa.ReduceOp.max).then_inc(max_made, 1)

            pool.memset(ones_col[:], 1.0).then_inc(col_made, 1)
            pool.wait_ge(col_made, 1)
            step(0, 0)
            step(1, 1)
            with pool.Fori(1, STEPS // 2) as i:
                step(2 * i, 0)
                step(2 * i + 1, 1)

        @block.scalar
        def _(act):
            def split_piece(g, i):
                act.wait_ge(raw_in[i % 2], 16 * (4 * g + i // 2 + 1))
                if not first(g):
                    if i < 4:
                        act.wait_ge(queries, 32 * g - 4 + i + 1)
                    else:
                        act.wait_ge(halves, 32 * g - 1 + (i - 4) // 2)
                act.activation(piece_of(wq_hi, wo_hi, i), piece_raw(i), ACT.Copy).then_inc(w_hi_made, 1)

            def query_hi(quad, quad_parity, p):
                act.wait_ge(queries, 4 * quad + p + 1)
                if p == 0 and not (isinstance(quad, int) and quad < 2):
                    act.wait_ge(scored, 4 * quad - 4)
                act.activation(q_hi[quad_parity][:, 2 * p:2 * p + 2, :],
                               ps_q[p % 2][:].rearrange("p (h t) -> p h t", h=2),
                               ACT.Copy).then_inc(q_hi_made, 1)

            def step(s, o, g):
                m, j = s.m, s.j
                if s.exp:
                    r = (j + 1) % 2
                    act.wait_ge(shifted, m)
                    if s.at_least(3):
                        act.wait_ge(weighted, m - 2)
                    act.activation(p_hi[r][:], s_sb[r][:], ACT.Exp, scale=SCALE)
                    act.activation(s_sb[r][:], s_sb[r][:], ACT.Exp, scale=SCALE).then_inc(exp_made, 1)
                if s.scores:
                    act.wait_ge(scored, m + 1)
                    if s.at_least(2):
                        act.wait_ge(p_lo_made, m - 1)
                    act.activation(s_sb[j % 2][:], ps_s[j % 2][:], ACT.Copy).then_inc(scores_copied, 1)
                if s.pv:
                    act.wait_ge(o_made, m - 1)
                    if j % 2 == 0 and s.at_least(6):
                        act.wait_ge(halves, m - 4)
                    token = slice(64 * (j % 2), 64 * (j % 2) + 64)
                    act.activation(o_hi[1 - s.pair_parity][:, :, token], o_sb[:],
                                   ACT.Copy).then_inc(o_hi_made, 1)
                if s.query:
                    query_hi(s.quad, (1 + j // 4) % 2, j % 4)
                for i in splits_at(o, j) if not isinstance(s.t, int) else []:
                    split_piece(g, i)

            for i in range(4):
                split_piece(0, i)
                query_hi(0, 0, i)
            for i in range(4, PIECES):
                split_piece(0, i)
            over_octets(act, lambda t, o, g: [step(Step(t, j), o, g) for j in range(8)])
            for j in range(4):
                step(Step(16, j), 0, NKV)

        @block.vector
        def _(dve):
            def split_piece(g, i):
                dve.wait_ge(w_hi_made, PIECES * g + i + 1)
                dve.tensor_tensor(piece_of(wq_lo, wo_lo, i), piece_raw(i), f32(piece_of(wq_hi, wo_hi, i)),
                                  ALU.subtract).then_inc(w_lo_made, 1)

            def query_lo(quad, quad_parity, p):
                dve.wait_ge(q_hi_made, 4 * quad + p + 1)
                dve.tensor_tensor(q_lo[quad_parity][:, 2 * p:2 * p + 2, :],
                                  ps_q[p % 2][:].rearrange("p (h t) -> p h t", h=2),
                                  f32(q_hi[quad_parity][:, 2 * p:2 * p + 2, :]),
                                  ALU.subtract).then_inc(q_lo_made, 1)

            def add_pair(s, tile):
                dve.wait_ge(halves, s.m - 4)
                dve.scalar_tensor_tensor(out=y[:, tile, :], in0=ps_y[:], scalar=gain[:], in1=y[:, tile, :],
                                         op0=ALU.mult, op1=ALU.add).then_inc(added, 1)

            def step(s, o, g):
                m, j = s.m, s.j
                if s.add:
                    tile = 4 * o - 3 + j // 2
                    add_pair(s, tile % TILES if isinstance(tile, int) else tile)
                if s.exp:
                    r = (j + 1) % 2
                    dve.wait_ge(max_made, m)
                    dve.tensor_tensor(s_sb[r][:], s_sb[r][:], s_max[r][:], ALU.subtract).then_inc(shifted, 1)
                if s.pv:
                    dve.wait_ge(summed, m - 1)
                    dve.tensor_reduce(sums[:], ps_sum[:].rearrange("p (k c) -> p k c", c=32), AX.X, ALU.max,
                                      apply_transpose=True).then_inc(sums_read, 1)
                    dve.wait_ge(sums_read, m - 1)
                    dve.reciprocal(rsums[:], sums[:]).then_inc(rsums_made, 1)
                    dve.wait_ge(rsums_made, m - 1)
                    dve.transpose(rsum_rows[:], rsums[:].unsqueeze(2).to_broadcast([P, 16, 32])
                                  ).then_inc(rsum_rows_made, 1)
                if s.exp:
                    dve.wait_ge(exp_made, m)
                    dve.tensor_tensor(p_lo[r][:], s_sb[r][:], f32(p_hi[r][:]), ALU.subtract).then_inc(p_lo_made, 1)
                if s.pv:
                    dve.wait_ge(rsum_rows_made, m - 1)
                    dve.wait_ge(weighted, m - 1)
                    dve.tensor_tensor(o_sb[:].rearrange("p h t -> p (h t)"), ps_o[j % 2][:], rsum_rows[:],
                                      ALU.mult).then_inc(o_made, 1)
                    dve.wait_ge(o_hi_made, m - 1)
                    token = slice(64 * (j % 2), 64 * (j % 2) + 64)
                    dve.tensor_tensor(o_lo[1 - s.pair_parity][:, :, token], o_sb[:],
                                      f32(o_hi[1 - s.pair_parity][:, :, token]), ALU.subtract).then_inc(o_lo_made, 1)
                if s.query:
                    query_lo(s.quad, (1 + j // 4) % 2, j % 4)
                for i in splits_at(o, j) if not isinstance(s.t, int) else []:
                    split_piece(g, i)

            for i in range(4):
                split_piece(0, i)
                query_lo(0, 0, i)
            for i in range(4, PIECES):
                split_piece(0, i)
            over_octets(dve, lambda t, o, g: [step(Step(t, j), o, g) for j in range(8)])
            for j in range(4):
                step(Step(16, j), 0, NKV)
            add_pair(Step(16, 4), TILES - 1)

        @block.tensor
        def _(pe):
            def project_queries(quad, quad_parity, p):
                for h in range(2):
                    for c in range(C):
                        n = slice((2 * p + h) * DH, (2 * p + h + 1) * DH)
                        last = three_pass(pe, ps_q[p % 2][:, 256 * h:256 * h + 256], wq_hi[:, c, n], wq_lo[:, c, n],
                                          xt[quad_parity][:, 0, c, :], xt[quad_parity][:, 1, c, :],
                                          c == 0, c == C - 1)
                last.then_inc(queries, 1)

            def step(s, o, g):
                t, m, j = s.t, s.m, s.j
                last_octet = isinstance(o, int) and o == 3
                if s.pv:
                    batch, r = (j + 2) % 4, j % 2
                    quad_parity = ((j + 6) // 4) % 2
                    if batch == 0:
                        pe.wait_ge(vt_in[quad_parity], 16 * (t + 1))
                    pe.wait_ge(p_lo_made, m - 1)
                    if s.at_least(3):
                        pe.wait_ge(sums_read, m - 2)
                    pe.matmul(ps_sum[:], ones_r[:], p_hi[r][:], start=True, stop=False)
                    pe.matmul(ps_sum[:], ones_r[:], p_lo[r][:], start=False, stop=True).then_inc(summed, 1)
                    if s.at_least(4):
                        pe.wait_ge(o_made, m - 3)
                    v = vt[quad_parity]
                    three_pass(pe, ps_o[r][:], v[:, batch, 0], v[:, batch, 1], p_hi[r][:], p_lo[r][:],
                               True, True).then_inc(weighted, 1)
                if s.scores:
                    batch, quad_parity = j % 4, j // 4
                    if batch == 0:
                        pe.wait_ge(kt_in[quad_parity], 16 * (t + 1))
                        pe.wait_ge(q_lo_made, 8 * t + 4 * quad_parity + 4)
                    if s.at_least(2):
                        pe.wait_ge(scores_copied, m - 1)
                    k = kt[quad_parity]
                    token = slice(64 * batch, 64 * batch + 64)
                    out = ps_s[j % 2][:].rearrange("p (h t) -> p h t", h=HG)
                    three_pass(pe, out, k[:, 0, batch], k[:, 1, batch], q_hi[quad_parity][:, :, token],
                               q_lo[quad_parity][:, :, token], True, True).then_inc(scored, 1)
                if s.query:
                    p, quad_parity = j % 4, (1 + j // 4) % 2
                    if p == 0:
                        pe.wait_ge(xt_in[quad_parity], 16 * (t + 1 + j // 4))
                    if last_octet and j >= 4:
                        pe.wait_ge(w_lo_made, PIECES * g + p + 1)
                    pe.wait_ge(q_lo_made, 4 * s.quad + p - 1)
                    project_queries(s.quad, quad_parity, p)
                if s.out:
                    half = j % 2
                    if half == 0:
                        pe.wait_ge(o_lo_made, m - 2)
                        if s.at_least(6):
                            pe.wait_ge(added, s.pair)
                    if isinstance(o, int) and o == 0 and j in (4, 5) and not (isinstance(t, int) and t == 16):
                        pe.wait_ge(w_lo_made, PIECES * g + 6 + 2 * half)
                    for h in range(4 * half, 4 * half + 4):
                        last = three_pass(pe, ps_y[:], o_hi[s.pair_parity][:, h, :], o_lo[s.pair_parity][:, h, :],
                                          wo_hi[:, h, :], wo_lo[:, h, :], h == 0, h == HG - 1)
                    last.then_inc(halves, 1)

            pe.wait_ge(xt_in[0], 16)
            for p in range(4):
                pe.wait_ge(w_lo_made, p + 1)
                if p >= 2:
                    pe.wait_ge(q_lo_made, p - 1)
                project_queries(0, 0, p)
            over_octets(pe, lambda t, o, g: [step(Step(t, j), o, g) for j in range(8)])
            for j in range(4):
                step(Step(16, j), 0, NKV)



EXPERTS = E + 2


def stage_three(nc, a, common, out):
    with ExitStack() as stack:
        b = Buffers(nc, stack)
        moe = {
            "x_hi": b.sb("x_hi", [P, C, T], F32R),
            "x_lo": b.sb("x_lo", [P, C, T], F32R),
            "gates": b.sb("gates3", [P, TILES, E + 1]),
            "gates_hi": b.sb("gates_hi", [E + 1, T], F32R),
            "gates_lo": b.sb("gates_lo", [E + 1, T], F32R),
            "b3_hi": b.sb("b3_hi", [E + 1, D], F32R),
            "b3_lo": b.sb("b3_lo", [E + 1, D], F32R),
            "bias_cols": b.sb("bias_cols", [P, 2, EXPERTS]),
        }
        route(nc, a, common, moe)
        experts(nc, a, common, moe, out)


def route(nc, a, common, moe):
    y, ident, gain = common["y"], common["ident"], common["gain_ffn"]
    x_hi, x_lo, gates = moe["x_hi"], moe["x_lo"], moe["gates"]
    gates_hi, gates_lo, b3_hi, b3_lo = moe["gates_hi"], moe["gates_lo"], moe["b3_hi"], moe["b3_lo"]
    bias_cols = moe["bias_cols"]
    with ExitStack() as stack:
        b = Buffers(nc, stack)
        stats = b.sb("stats3", [P, TILES, 6])
        mean_var = b.sb("mean_var3", [P, TILES, 2])
        std = b.sb("std3", [P, TILES])
        rstd = b.sb("rstd3", [P, TILES])
        eps = b.sb("eps3", [P, 1])
        normed = [b.sb(f"normed3_{i}", [P, D]) for i in range(2)]
        rw_raw = b.sb("rw_raw", [P, C, E])
        rw_hi = b.sb("rw_hi", [P, C, E], F32R)
        rw_lo = b.sb("rw_lo", [P, C, E], F32R)
        rb = b.sb("rb", [E, 1])
        rbias = b.sb("rbias", [P, E])
        b3_raw = b.sb("b3_raw", [E + 1, D])
        bias_rows = b.sb("bias_rows", [2 * EXPERTS, P])
        logits_t = b.sb("logits_t", [E, T])
        logits = b.sb("logits", [P, TILES, E])
        probs = b.sb("probs", [P, TILES, E])
        scores = b.sb("scores", [P, TILES, E])
        masked = b.sb("masked", [P, TILES, E])
        marks = b.sb("marks", [P, TILES, E])
        chosen = b.sb("chosen", [P, TILES, E])
        row = b.sb("row", [P, TILES])
        group_max = b.sb("group_max", [P, TILES, GROUPS])
        rank = b.sb("rank", [P, TILES, GROUPS])
        beats = b.sb("beats", [P, TILES])
        order = b.sb("order", [P, E])
        ps_t = [b.ps(f"ps3_t{i}", [P, C, P]) for i in range(2)]
        ps_l = b.ps("ps_l", [E, 512])
        ps_turn = b.ps("ps_turn", [P, 512])
        ps_g = [b.ps(f"ps_g{i}", [E + 1, 512]) for i in range(4)]

        small_in = b.sem("small_in")
        consts_made = b.sem("consts3_made")
        stats_made = b.sem("stats3_made")
        meanvar_made = b.sem("meanvar3_made")
        std_made = b.sem("std3_made")
        rstd_made = b.sem("rstd3_made")
        normed_made = b.sem("normed3_made")
        transposed = b.sem("transposed3")
        x_hi_made = b.sem("x_hi_made")
        x_lo_made = b.sem("x_lo_made")
        small_hi_made = b.sem("small_hi_made")
        small_lo_made = b.sem("small_lo_made")
        logits_t_done = b.sem("logits_t_done")
        logits_t_copied = b.sem("logits_t_copied")
        logits_turned = b.sem("logits_turned")
        bias_turned = b.sem("bias_turned")
        bias_copied = b.sem("bias_copied")
        routed = b.sem("routed")
        logits_shifted = b.sem("logits_shifted")
        exp_made = b.sem("exp3_made")
        gates_made = b.sem("gates_made")
        gates_turned = b.sem("gates_turned")
        gates_hi_made = b.sem("gates_hi_made")
        gates_lo_made = b.sem("gates_lo_made")

        line = lambda name: a[name].rearrange("(a b) -> a b", a=1)
        small = [(rw_raw[:], a["L0_ffn_router_w"].rearrange("(c p) e -> p c e", p=P)),
                 (rb[:], a["L0_ffn_router_b"].rearrange("(e a) -> e a", a=1)),
                 (rbias[:], line("L0_ffn_router_bias").to_broadcast([P, E])),
                 (b3_raw[0:E], a["L0_ffn_eb3"]),
                 (b3_raw[E:E + 1], line("L0_ffn_sb3")),
                 (bias_rows[0:2], a["L0_ffn_sb1"].rearrange("(s n) -> s n", s=2)),
                 (bias_rows[2:EXPERTS], a["L0_ffn_eb1"]),
                 (bias_rows[EXPERTS:EXPERTS + 2], a["L0_ffn_sb2"].rearrange("(s n) -> s n", s=2)),
                 (bias_rows[EXPERTS + 2:2 * EXPERTS], a["L0_ffn_eb2"])]
        SMALL = 16 * len(small)

        block = stack.enter_context(nc.Block())

        @block.sync
        def _(sp):
            for dst, src in small:
                sp.dma_start(dst, src).then_inc(small_in, 16)

        @block.gpsimd
        def _(pool):
            pool.memset(eps[:], EPS).then_inc(consts_made, 1)
            pool.iota(order[:], pattern=[[-1, E]], base=E, channel_multiplier=0,
                      allow_small_or_imprecise_dtypes=True).then_inc(consts_made, 1)

        @block.scalar
        def _(act):
            act.wait_ge(small_in, SMALL)
            act.activation(rw_hi[:], rw_raw[:], ACT.Copy).then_inc(small_hi_made, 1)
            act.activation(b3_hi[:], b3_raw[:], ACT.Copy).then_inc(small_hi_made, 1)
            act.wait_ge(consts_made, 2)

            def x_high(n):
                act.wait_ge(transposed, n + 1)
                act.activation(x_hi[:, :, n * P:(n + 1) * P], ps_t[n % 2][:], ACT.Copy).then_inc(x_hi_made, 1)

            for o in range(OCTETS):
                tiles = slice(4 * o, 4 * o + 4)
                act.wait_ge(meanvar_made, 4 * o + 4)
                act.activation(std[:, tiles], mean_var[:, tiles, 1], ACT.Sqrt, bias=eps[:]).then_inc(std_made, 1)
                for n in range(4 * o, 4 * o + 4):
                    x_high(n)
                act.wait_ge(logits_t_done, o + 1)
                act.activation(logits_t[:, 512 * o:512 * o + 512], ps_l[:], ACT.Identity,
                               bias=rb[:]).then_inc(logits_t_copied, 1)
            act.wait_ge(logits_shifted, 1)
            act.activation(probs[:], marks[:], ACT.Exp).then_inc(exp_made, 1)
            for i in range(4):
                act.wait_ge(gates_turned, i + 1)
                act.activation(gates_hi[:, 512 * i:512 * i + 512], ps_g[i][:], ACT.Copy).then_inc(gates_hi_made, 1)

        @block.vector
        def _(dve):
            def stats_of(lo, hi):
                for n in range(lo, hi):
                    dve.bn_stats(stats[:, n, :], y[:, n, :]).then_inc(stats_made, 1)
                for n in range(lo, hi):
                    dve.wait_ge(stats_made, n + 1)
                    dve.bn_aggr(mean_var[:, n, :], stats[:, n, :]).then_inc(meanvar_made, 1)

            def normalise(n):
                if n >= 2:
                    dve.wait_ge(transposed, n - 1)
                dve.tensor_scalar(normed[n % 2][:], y[:, n, :], mean_var[:, n, 0:1], rstd[:, n:n + 1],
                                  ALU.subtract, ALU.mult).then_inc(normed_made, 1)

            def x_low(n):
                dve.wait_ge(x_hi_made, n + 1)
                tokens = slice(n * P, (n + 1) * P)
                dve.tensor_tensor(x_lo[:, :, tokens], ps_t[n % 2][:], f32(x_hi[:, :, tokens]),
                                  ALU.subtract).then_inc(x_lo_made, 1)

            stats_of(0, 4)
            dve.wait_ge(bias_turned, 1)
            dve.tensor_copy(bias_cols[:].rearrange("p i e -> p (i e)"),
                            ps_turn[:, 256:256 + 2 * EXPERTS]).then_inc(bias_copied, 1)
            for i, (lo, raw, hi) in enumerate(((rw_lo, rw_raw, rw_hi), (b3_lo, b3_raw, b3_hi))):
                dve.wait_ge(small_hi_made, i + 1)
                dve.tensor_tensor(lo[:], raw[:], f32(hi[:]), ALU.subtract).then_inc(small_lo_made, 1)
            for o in range(OCTETS):
                tiles = slice(4 * o, 4 * o + 4)
                dve.wait_ge(std_made, o + 1)
                dve.reciprocal(rstd[:, tiles], std[:, tiles]).then_inc(rstd_made, 1)
                dve.wait_ge(rstd_made, o + 1)
                normalise(4 * o)
                normalise(4 * o + 1)
                x_low(4 * o)
                normalise(4 * o + 2)
                x_low(4 * o + 1)
                normalise(4 * o + 3)
                x_low(4 * o + 2)
                x_low(4 * o + 3)
                if o + 1 < OCTETS:
                    stats_of(4 * o + 4, 4 * o + 8)

            count = [0]

            def link(ins):
                count[0] += 1
                ins.then_inc(routed, 1)
                dve.wait_ge(routed, count[0])

            def spread(v, width):
                return v.unsqueeze(2).to_broadcast([P, TILES, width])

            def along(v):
                return v.unsqueeze(1).to_broadcast([P, TILES, E])

            def by_group(v):
                return v[:].rearrange("p n (g k) -> p (n g) k", g=GROUPS)

            def group_spread(v):
                return v[:].rearrange("p n g -> p (n g)").unsqueeze(2).to_broadcast([P, TILES * GROUPS, E // GROUPS])

            def take_best(first_choice):
                link(dve.tensor_reduce(row[:], masked[:], AX.X, ALU.max))
                link(dve.tensor_tensor(marks[:], masked[:], spread(row[:], E), ALU.is_equal))
                link(dve.tensor_tensor(marks[:], marks[:], along(order[:]), ALU.mult))
                link(dve.tensor_reduce(row[:], marks[:], AX.X, ALU.max))
                if first_choice:
                    link(dve.tensor_tensor(chosen[:], marks[:], spread(row[:], E), ALU.is_equal))
                    link(dve.scalar_tensor_tensor(out=masked[:], in0=chosen[:], scalar=LOWEST, in1=masked[:],
                                                  op0=ALU.mult, op1=ALU.add))
                else:
                    link(dve.tensor_tensor(marks[:], marks[:], spread(row[:], E), ALU.is_equal))
                    link(dve.tensor_tensor(chosen[:], chosen[:], marks[:], ALU.add))

            dve.wait_ge(logits_turned, 1)
            link(dve.tensor_copy(logits[:].rearrange("p n e -> p (n e)"), ps_turn[:, 0:TILES * E]))
            link(dve.tensor_reduce(row[:], logits[:], AX.X, ALU.max))
            dve.tensor_tensor(marks[:], logits[:], spread(row[:], E), ALU.subtract).then_inc(logits_shifted, 1)
            for g in range(GROUPS):
                link(dve.memset(rank[:, :, g], float(GROUPS - 1 - g)))
            dve.wait_ge(exp_made, 1)
            link(dve.tensor_reduce(row[:], probs[:], AX.X, ALU.add))
            link(dve.reciprocal(row[:], row[:]))
            link(dve.tensor_tensor(probs[:], probs[:], spread(row[:], E), ALU.mult))
            link(dve.tensor_tensor(scores[:], probs[:], along(rbias[:]), ALU.add))
            link(dve.tensor_reduce(group_max[:].rearrange("p n g -> p (n g)"), by_group(scores), AX.X, ALU.max))
            for g in range(GROUPS):
                for later in range(g + 1, GROUPS):
                    link(dve.tensor_tensor(beats[:], group_max[:, :, g], group_max[:, :, later], ALU.is_ge))
                    dve.tensor_tensor(rank[:, :, g], rank[:, :, g], beats[:], ALU.subtract)
                    link(dve.tensor_tensor(rank[:, :, later], rank[:, :, later], beats[:], ALU.add))
            link(dve.tensor_scalar(rank[:], rank[:], 2.0, None, ALU.is_lt))
            link(dve.tensor_tensor(by_group(masked), by_group(scores), group_spread(rank), ALU.mult))
            link(dve.tensor_scalar(rank[:], rank[:], 1.0, -LOWEST, ALU.subtract, ALU.mult))
            link(dve.tensor_tensor(by_group(masked), by_group(masked), group_spread(rank), ALU.add))
            take_best(True)
            take_best(False)
            link(dve.memset(marks[:, :, 0:1], 1.0))
            dve.scalar_tensor_tensor(out=gates[:, :, 0:E], in0=scores[:], scalar=gain[:], in1=chosen[:],
                                     op0=ALU.mult, op1=ALU.mult).then_inc(gates_made, 1)
            dve.tensor_scalar(gates[:, :, E:E + 1], marks[:, :, 0:1], gain[:], None, ALU.mult).then_inc(gates_made, 1)
            for i in range(4):
                dve.wait_ge(gates_hi_made, i + 1)
                tokens = slice(512 * i, 512 * i + 512)
                dve.tensor_tensor(gates_lo[:, tokens], ps_g[i][:], f32(gates_hi[:, tokens]),
                                  ALU.subtract).then_inc(gates_lo_made, 1)

        @block.tensor
        def _(pe):
            pe.wait_ge(small_in, SMALL)
            pe.transpose(ps_turn[:, 256:256 + 2 * EXPERTS], bias_rows[:], ident[0:2 * EXPERTS, 0:2 * EXPERTS]
                         ).then_inc(bias_turned, 1)
            pe.wait_ge(small_lo_made, 1)

            def octet_logits(o):
                pe.wait_ge(x_lo_made, 4 * o + 4)
                if o:
                    pe.wait_ge(logits_t_copied, o)
                tokens = slice(512 * o, 512 * o + 512)
                for c in range(C):
                    last = three_pass(pe, ps_l[:], rw_hi[:, c, :], rw_lo[:, c, :], x_hi[:, c, tokens],
                                      x_lo[:, c, tokens], c == 0, c == C - 1)
                last.then_inc(logits_t_done, 1)

            for n in range(TILES):
                pe.wait_ge(normed_made, n + 1)
                if n >= 2:
                    pe.wait_ge(x_lo_made, n - 1)
                for c in range(C):
                    last = pe.transpose(ps_t[n % 2][:, c, :], normed[n % 2][:, c * P:(c + 1) * P], ident[:])
                last.then_inc(transposed, 1)
                if n % 4 == 3:
                    octet_logits(n // 4)
            pe.wait_ge(logits_t_copied, OCTETS)
            pe.wait_ge(bias_copied, 1)
            for n in range(TILES):
                last = pe.transpose(ps_turn[:, n * E:(n + 1) * E], logits_t[:, n * P:(n + 1) * P], ident[0:E, 0:E])
            last.then_inc(logits_turned, 1)
            pe.wait_ge(gates_made, 2)
            for n in range(TILES):
                last = pe.transpose(ps_g[n // 4][:, (n % 4) * P:(n % 4 + 1) * P], gates[:, n, :], ident[:])
                if n % 4 == 3:
                    last.then_inc(gates_turned, 1)


def experts(nc, a, common, moe, out):
    y = common["y"]
    x_hi, x_lo, gates, bias_cols = moe["x_hi"], moe["x_lo"], moe["gates"], moe["bias_cols"]
    gates_hi, gates_lo, b3_hi, b3_lo = moe["gates_hi"], moe["gates_lo"], moe["b3_hi"], moe["b3_lo"]
    with ExitStack() as stack:
        b = Buffers(nc, stack)
        w_raw = [b.sb(f"w3_raw{i}", [P, 3, 512]) for i in range(2)]
        w_hi = [b.sb(f"w3_hi{i}", [P, 3, 512], F32R) for i in range(2)]
        w_lo = [b.sb(f"w3_lo{i}", [P, 3, 512], F32R) for i in range(2)]
        biases = [b.sb(f"biases{i}", [P, 2]) for i in range(2)]
        silu = [b.sb(f"silu{i}", [P, 512]) for i in range(2)]
        h_sb = [b.sb(f"h_sb{i}", [P, 512]) for i in range(2)]
        h_hi = [b.sb(f"h_hi{i}", [P, 512], F32R) for i in range(2)]
        h_lo = [b.sb(f"h_lo{i}", [P, 512], F32R) for i in range(2)]
        ps_up = [[b.ps(f"ps_up{i}{k}", [P, 512]) for k in range(2)] for i in range(2)]
        ps_down = [b.ps(f"ps_down{i}", [P, 512]) for i in range(4)]

        raw_in = [b.sem(f"raw3_in{i}") for i in range(2)]
        w_hi_made = b.sem("w3_hi_made")
        w_lo_made = b.sem("w3_lo_made")
        up_done = b.sem("up_done")
        silu_made = b.sem("silu_made")
        h_made = b.sem("h_made")
        h_hi_made = b.sem("h_hi_made")
        h_lo_made = b.sem("h_lo_made")
        down_done = b.sem("down_done")
        y_added = b.sem("y_added")
        stored = b.sem("stored")

        out_v = out.rearrange("b s d -> (b s) d").rearrange("(o i p) d -> o p i d", i=4, p=P)
        block = stack.enter_context(nc.Block())

        @block.sync
        def _(sp):
            def load(e, parity):
                if not (isinstance(e, int) and e < 2):
                    sp.wait_ge(w_lo_made, e - 1)
                    up = [a["L0_ffn_ew1"][e - 2], a["L0_ffn_ew2"][e - 2]]
                    down = a["L0_ffn_ew3"][e - 2]
                else:
                    n = slice(INTER * e, INTER * e + INTER)
                    up = [a["L0_ffn_sw1"][:, n], a["L0_ffn_sw2"][:, n]]
                    down = a["L0_ffn_sw3"][n, :]
                for i in range(2):
                    sp.dma_start(w_raw[parity][:, i].rearrange("p (c n) -> p c n", c=C),
                                 up[i].rearrange("(c p) n -> p c n", p=P)).then_inc(raw_in[parity], 16)
                sp.dma_start(w_raw[parity][:, 2], down).then_inc(raw_in[parity], 16)

            load(0, 0)
            load(1, 1)
            with sp.Fori(1, EXPERTS // 2) as k:
                load(2 * k, 0)
                load(2 * k + 1, 1)
            for o in range(OCTETS):
                sp.wait_ge(y_added, TILES * EXPERTS + 4 * o + 4)
                sp.dma_start(out_v[o], y[:, 4 * o:4 * o + 4, :]).then_inc(stored, 16)
            sp.wait_ge(stored, 16 * OCTETS)

        @block.scalar
        def _(act):
            def split_hi(e, parity):
                act.wait_ge(raw_in[parity], 48 * ((e - parity) // 2 + 1) if isinstance(e, int) else 24 * (e - parity) + 48)
                if not (isinstance(e, int) and e < 2):
                    act.wait_ge(down_done, TILES * e)
                act.activation(w_hi[parity][:], w_raw[parity][:], ACT.Copy).then_inc(w_hi_made, 1)

            def expert(e, parity, more=True):
                for o in range(OCTETS):
                    r = o % 2
                    q = 4 * e + o
                    early = isinstance(q, int) and q < 2
                    act.wait_ge(up_done, q + 1)
                    if not early:
                        act.wait_ge(h_made, q - 1)
                    act.activation(silu[r][:], ps_up[r][0][:], ACT.Silu, bias=biases[parity][:, 0:1]).then_inc(silu_made, 1)
                    act.wait_ge(h_made, q + 1)
                    if not early:
                        act.wait_ge(down_done, TILES + 4 * q - 4)
                    act.activation(h_hi[r][:], h_sb[r][:], ACT.Copy).then_inc(h_hi_made, 1)
                    if o == 1 and more:
                        split_hi(e + 1, 1 - parity)

            split_hi(0, 0)
            expert(0, 0)
            expert(1, 1)
            with act.Fori(1, EXPERTS // 2 - 1) as k:
                expert(2 * k, 0)
                expert(2 * k + 1, 1)
            expert(EXPERTS - 2, 0)
            expert(EXPERTS - 1, 1, more=False)

        @block.vector
        def _(dve):
            def split_lo(e, parity):
                dve.wait_ge(w_hi_made, e + 1)
                dve.tensor_tensor(w_lo[parity][:], w_raw[parity][:], f32(w_hi[parity][:]), ALU.subtract)
                column = slice(e, e + 1) if isinstance(e, int) else bass.ds(e, 1)
                dve.tensor_copy(biases[parity][:], bias_cols[:, :, column].rearrange("p i a -> p (i a)")
                                ).then_inc(w_lo_made, 1)

            def add_tile(o, i, count, gate):
                dve.wait_ge(down_done, count)
                n = 4 * o + i
                if gate is None:
                    ins = dve.tensor_tensor(y[:, n, :], ps_down[i][:], y[:, n, :], ALU.add)
                else:
                    ins = dve.scalar_tensor_tensor(out=y[:, n, :], in0=ps_down[i][:], scalar=gate(n),
                                                   in1=y[:, n, :], op0=ALU.mult, op1=ALU.add)
                ins.then_inc(y_added, 1)

            def gate_of(e):
                if isinstance(e, int) and e < 2:
                    return lambda n: gates[:, n, E:E + 1]
                if isinstance(e, int):
                    return lambda n: gates[:, n, e - 2:e - 1]
                return lambda n: gates[:, n, bass.ds(e - 2, 1)]

            def expert(e, parity, gate_before, more=True):
                for o in range(OCTETS):
                    r = o % 2
                    q = 4 * e + o
                    if not (isinstance(q, int) and q < 2):
                        dve.wait_ge(h_lo_made, q - 1)
                    dve.wait_ge(silu_made, q + 1)
                    dve.scalar_tensor_tensor(out=h_sb[r][:], in0=ps_up[r][1][:], scalar=biases[parity][:, 1:2], in1=silu[r][:],
                                             op0=ALU.add, op1=ALU.mult).then_inc(h_made, 1)
                    if not (isinstance(q, int) and q == 0):
                        for i in range(4):
                            add_tile((o - 1) % 4, i, TILES + 4 * q - 4 + i + 1, gate_of(e) if o else gate_before)
                    dve.wait_ge(h_hi_made, q + 1)
                    dve.tensor_tensor(h_lo[r][:], h_sb[r][:], f32(h_hi[r][:]), ALU.subtract).then_inc(h_lo_made, 1)
                    if o == 1 and more:
                        split_lo(e + 1, 1 - parity)

            split_lo(0, 0)
            for n in range(TILES):
                add_tile(n // 4, n % 4, n + 1, None)
            expert(0, 0, None)
            expert(1, 1, gate_of(0))
            expert(2, 0, gate_of(1))
            expert(3, 1, gate_of(2))
            with dve.Fori(2, EXPERTS // 2 - 1) as k:
                expert(2 * k, 0, gate_of(2 * k - 1))
                expert(2 * k + 1, 1, gate_of(2 * k))
            expert(EXPERTS - 2, 0, gate_of(EXPERTS - 3))
            expert(EXPERTS - 1, 1, gate_of(EXPERTS - 2), more=False)
            for i in range(4):
                add_tile(3, i, TILES + 16 * EXPERTS - 4 + i + 1, gate_of(EXPERTS - 1))

        @block.tensor
        def _(pe):
            def up(e, parity, o):
                r = o % 2
                q = 4 * e + o
                if o == 0:
                    pe.wait_ge(w_lo_made, e + 1)
                if not (isinstance(q, int) and q < 2):
                    pe.wait_ge(h_made, q - 1)
                tokens = slice(512 * o, 512 * o + 512)
                for k in range(2):
                    for c in range(C):
                        n = slice(INTER * c, INTER * c + INTER)
                        last = three_pass(pe, ps_up[r][k][:], w_hi[parity][:, k, n], w_lo[parity][:, k, n],
                                          x_hi[:, c, tokens], x_lo[:, c, tokens], c == 0, c == C - 1)
                last.then_inc(up_done, 1)

            def down(q, r, parity):
                pe.wait_ge(h_lo_made, q + 1)
                for i in range(4):
                    pe.wait_ge(y_added, TILES + 4 * q - 4 + i + 1)
                    tokens = slice(P * i, P * i + P)
                    three_pass(pe, ps_down[i][:], h_hi[r][:, tokens], h_lo[r][:, tokens], w_hi[parity][:, 2],
                               w_lo[parity][:, 2], True, True).then_inc(down_done, 1)

            def expert(e, parity):
                for o in range(OCTETS):
                    up(e, parity, o)
                    if o:
                        down(4 * e + o - 1, (o - 1) % 2, parity)
                    elif not first(e):
                        down(4 * e - 1, 1, 1 - parity)

            for n in range(TILES):
                if n >= 4:
                    pe.wait_ge(y_added, n - 3)
                tokens = slice(P * n, P * n + P)
                three_pass(pe, ps_down[n % 4][:], gates_hi[:, tokens], gates_lo[:, tokens], b3_hi[:], b3_lo[:],
                           True, True).then_inc(down_done, 1)
            expert(0, 0)
            expert(1, 1)
            with pe.Fori(1, EXPERTS // 2) as k:
                expert(2 * k, 0)
                expert(2 * k + 1, 1)
            down(4 * EXPERTS - 1, 1, 1)


INS = ['x', 'ctx_4096', 'g_xattn', 'g_ffn', 'L0_xattn_Wq', 'L0_xattn_Wk', 'L0_xattn_Wv', 'L0_xattn_Wo',
       'L0_ffn_router_w', 'L0_ffn_router_b', 'L0_ffn_router_bias', 'L0_ffn_ew1', 'L0_ffn_eb1',
       'L0_ffn_ew2', 'L0_ffn_eb2', 'L0_ffn_ew3', 'L0_ffn_eb3', 'L0_ffn_sw1', 'L0_ffn_sb1',
       'L0_ffn_sw2', 'L0_ffn_sb2', 'L0_ffn_sw3', 'L0_ffn_sb3']


def program(nc, a, out):
    scratch = {
        "x": nc.dram_tensor("x_scratch", (QUADS, P, 2, C, 256), F32, kind="Internal").ap(),
        "k": nc.dram_tensor("k_scratch", (NKV, QUADS, P, 2 * QB * KEYS), F32, kind="Internal").ap(),
        "v": nc.dram_tensor("v_scratch", (NKV, QUADS, KEYS, QB, 2, DH), F32, kind="Internal").ap(),
    }
    with ExitStack() as stack:
        b = Buffers(nc, stack)
        common = {
            "y": b.sb("y", [P, TILES, D]),
            "ident": b.sb("ident", [P, P]),
            "ones_r": b.sb("ones_r", [P, P], F32R),
            "gain_attn": b.sb("gain_attn", [P, 1]),
            "gain_ffn": b.sb("gain_ffn", [P, 1]),
        }
        stage_one(nc, a, common, scratch)
        stage_two(nc, a, common, scratch)
        stage_three(nc, a, common, out)


def kernel(**inputs):
    import concourse.bacc as bacc
    from concourse.bass_utils import run_bass_kernel_spmd as run

    nc = bacc.Bacc("TRN2", target_bir_lowering=False, num_devices=1)
    arrays, args = {}, {}
    for name in INS:
        arr = np.ascontiguousarray(inputs[name])
        arrays[f"in_{name}"] = arr
        args[name] = nc.dram_tensor(f"in_{name}", arr.shape, mybir.dt.from_np(arr.dtype),
                                    kind="ExternalInput").ap()
    out = nc.dram_tensor("out_0", (BATCH, SQ, D), F32, kind="ExternalOutput").ap()
    program(nc, args, out)
    r = run(nc, [arrays], core_ids=[0])
    return r.results[0]["out_0"]
```

```python
from contextlib import ExitStack

import numpy as np
import concourse.bass as bass
import concourse.mybir as mybir
from concourse.alu_op_type import AluOpType as ALU

ACT = mybir.ActivationFunctionType
AX = mybir.AxisListType
F32 = mybir.dt.float32
F32R = mybir.dt.float32r

P = 128
BATCH = 32
SQ = 64
SC = 64
D = 512
C = D // P
DH = 128
NKV = 4
HG = 8
T = BATCH * SQ
TILES = T // P
OCTETS = T // 512
QUADS = T // 256
QB = 4
KEYS = SQ + SC
E = 16
GROUPS = 4
INTER = 128
EPS = 1e-5
SCALE = DH ** -0.5
LOWEST = -3.0e38


class Buffers:

    def __init__(self, nc, stack):
        self.nc, self.stack = nc, stack

    def sb(self, name, shape, dt=F32):
        return self.stack.enter_context(self.nc.sbuf_tensor(name, shape, dt))

    def ps(self, name, shape, dt=F32):
        return self.stack.enter_context(self.nc.psum_tensor(name, shape, dt))

    def sem(self, name):
        return self.stack.enter_context(self.nc.semaphore(name))


def f32(ap):
    return ap.bitcast(F32)


def first(i):
    return isinstance(i, int) and i == 0


def three_pass(pe, out, w_hi, w_lo, x_hi, x_lo, first, last):
    pe.matmul(out, w_hi, x_hi, start=first, stop=False)
    pe.matmul(out, w_lo, x_hi, start=False, stop=False)
    return pe.matmul(out, w_hi, x_lo, start=False, stop=last)



def stage_one(nc, a, common, scratch):
    y, ident, ones_r = common["y"], common["ident"], common["ones_r"]
    gain_attn, gain_ffn = common["gain_attn"], common["gain_ffn"]
    with ExitStack() as stack:
        b = Buffers(nc, stack)
        ctx_raw = b.sb("ctx_raw", [P, 4, D])
        kv_raw = b.sb("kv_raw", [P, 2, C, D])
        wk_hi = b.sb("wk_hi", [P, C, D], F32R)
        wk_lo = b.sb("wk_lo", [P, C, D], F32R)
        wv_hi = b.sb("wv_hi", [P, C, D], F32R)
        wv_lo = b.sb("wv_lo", [P, C, D], F32R)
        tok_hi = b.sb("tok_hi", [P, 2, C, 512], F32R)
        tok_lo = b.sb("tok_lo", [P, 2, C, 512], F32R)
        k_out = [b.sb(f"k_out{i}", [P, 2, 2, QB, KEYS], F32R) for i in range(2)]
        v_out = [b.sb(f"v_out{i}", [P, NKV, 2, DH], F32R) for i in range(2)]
        normed = [b.sb(f"normed{i}", [P, D]) for i in range(2)]
        stats = b.sb("stats", [P, TILES, 6])
        mean_var = b.sb("mean_var", [P, TILES, 2])
        std = b.sb("std", [P, TILES])
        rstd = b.sb("rstd", [P, TILES])
        gates = b.sb("gates", [P, 2])
        eps = b.sb("eps", [P, 1])
        ones = b.sb("ones", [P, P])
        ps_t = [b.ps(f"ps_t{i}", [P, C, P]) for i in range(2)]
        ps_a = [b.ps(f"ps_a{i}", [P, 512]) for i in range(2)]

        x_in = b.sem("x_in")
        ctx_in = b.sem("ctx_in")
        kv_in = b.sem("kv_in")
        gates_in = b.sem("gates_in")
        consts_made = b.sem("consts_made")
        ones_copied = b.sem("ones_copied")
        gains_made = b.sem("gains_made")
        stats_made = b.sem("stats_made")
        meanvar_made = b.sem("meanvar_made")
        std_made = b.sem("std_made")
        rstd_made = b.sem("rstd_made")
        normed_made = b.sem("normed_made")
        kv_hi_made = b.sem("kv_hi_made")
        kv_lo_made = b.sem("kv_lo_made")
        transposed = b.sem("transposed")
        tok_hi_made = b.sem("tok_hi_made")
        tok_lo_made = b.sem("tok_lo_made")
        projected = b.sem("projected")
        out_hi_made = b.sem("out_hi_made")
        out_lo_made = b.sem("out_lo_made")
        k_stored = [b.sem(f"k_stored{i}") for i in range(2)]
        v_stored = [b.sem(f"v_stored{i}") for i in range(2)]
        x_stored = b.sem("x_stored")

        x_v = a["x"].rearrange("b s d -> (b s) d").rearrange("(o i p) d -> o p i d", i=4, p=P)
        ctx_v = a["ctx_4096"].rearrange("b s d -> (b s) d").rearrange("(o i p) d -> o p i d", i=4, p=P)
        UNITS = 8
        JOBS = 16

        block = stack.enter_context(nc.Block())

        @block.sync
        def _(sp):
            sp.dma_start(kv_raw[:, 0], a["L0_xattn_Wv"].rearrange("(c p) n -> p c n", p=P)).then_inc(kv_in, 16)
            sp.dma_start(ctx_raw[:], ctx_v[0]).then_inc(ctx_in, 16)
            sp.dma_start(y[:, 0:4, :], x_v[0]).then_inc(x_in, 16)
            sp.wait_ge(kv_in, 16)
            sp.dma_start(kv_raw[:, 1], a["L0_xattn_Wk"].rearrange("(c p) n -> p c n", p=P)).then_inc(kv_in, 16)
            for o in range(1, OCTETS):
                sp.wait_ge(x_in, 16 * o)
                sp.dma_start(y[:, 4 * o:4 * o + 4, :], x_v[o]).then_inc(x_in, 16)

            def octet(o, more):
                for u in range(UNITS):
                    src, i = u % 2, u // 2
                    if u == 7:
                        if more:
                            sp.wait_ge(transposed, UNITS * o + 7)
                            sp.dma_start(ctx_raw[:], ctx_v[o + 1]).then_inc(ctx_in, 16)
                    sp.wait_ge(out_lo_made, JOBS * o + u + 1)
                    for bb in range(2):
                        batch = (i % 2) * 2 + bb
                        dst = scratch["v"][:, 2 * o + i // 2, src * 64:src * 64 + 64, batch]
                        sp.dma_start(dst.rearrange("g t h d -> t g (h d)"),
                                     f32(v_out[u % 2][64 * bb:64 * bb + 64]).rearrange("t g h d -> t g (h d)")
                                     ).then_inc(v_stored[u % 2], 16)
                for half in range(2):
                    for s, tok in enumerate((tok_hi, tok_lo)):
                        sp.dma_start(scratch["x"][2 * o + half, :, s],
                                     f32(tok[:, 1, :, 256 * half:256 * half + 256])).then_inc(x_stored, 16)
                for g in range(NKV):
                    sp.wait_ge(out_lo_made, JOBS * o + UNITS + 2 * g + 2)
                    sp.dma_start(scratch["k"][g, bass.ds(2 * o, 2)].rearrange("q p n -> p q n"),
                                 f32(k_out[g % 2][:]).rearrange("p q h b k -> p q (h b k)")
                                 ).then_inc(k_stored[g % 2], 16)

            with sp.Fori(0, OCTETS - 1) as o:
                octet(o, True)
            octet(OCTETS - 1, False)
            for i in range(2):
                sp.wait_ge(k_stored[i], 16 * OCTETS * NKV // 2)
                sp.wait_ge(v_stored[i], 16 * OCTETS * UNITS)
            sp.wait_ge(x_stored, 16 * 4 * OCTETS)

        @block.gpsimd
        def _(pool):
            pool.memset(ident[:], 0.0).then_inc(consts_made, 1)
            pool.memset(ones[:], 1.0).then_inc(consts_made, 1)
            pool.memset(eps[:], EPS).then_inc(consts_made, 1)
            pool.wait_ge(consts_made, 3)
            pool.affine_select(out=ident[:], in_=ident[:], compare_op=ALU.not_equal, fill=1.0, base=0,
                               pattern=[[-1, P]], channel_multiplier=1).then_inc(consts_made, 1)
            for i, name in enumerate(("g_xattn", "g_ffn")):
                src = a[name].rearrange("(a b) -> a b", a=1).to_broadcast([P, 1])
                pool.dma_start(gates[:, i:i + 1], src).then_inc(gates_in, 16)

        @block.scalar
        def _(act):
            def std_of(lo, hi):
                act.wait_ge(meanvar_made, hi)
                act.activation(std[:, lo:hi], mean_var[:, lo:hi, 1], ACT.Sqrt, bias=eps[:]).then_inc(std_made, 1)

            def split_hi(i, hi):
                act.wait_ge(kv_in, 16 * (i + 1))
                act.activation(hi[:], kv_raw[:, i], ACT.Copy).then_inc(kv_hi_made, 1)

            split_hi(0, wv_hi)

            def octet(o):
                def tok(u):
                    src, i = u % 2, u // 2
                    act.wait_ge(transposed, UNITS * o + u + 1)
                    if u == 0 and not first(o):
                        act.wait_ge(x_stored, 64 * o)
                    act.activation(tok_hi[:, src, :, i * P:(i + 1) * P], ps_t[u % 2][:],
                                   ACT.Copy).then_inc(tok_hi_made, 1)

                def v_job(u):
                    act.wait_ge(projected, JOBS * o + u + 1)
                    if not (first(o) and u < 2):
                        act.wait_ge(v_stored[u % 2], 32 * (4 * o + u // 2))
                    act.activation(v_out[u % 2][:, :, 0, :], ps_a[u % 2][:].rearrange("p (g d) -> p g d", g=NKV),
                                   ACT.Copy).then_inc(out_hi_made, 1)

                tok(0)
                if first(o):
                    act.wait_ge(consts_made, 4)
                    act.wait_ge(gates_in, 32)
                    act.activation(gain_attn[:], gates[:, 0:1], ACT.Tanh).then_inc(gains_made, 1)
                    act.activation(gain_ffn[:], gates[:, 1:2], ACT.Tanh).then_inc(gains_made, 1)
                    act.activation(ones_r[:], ones[:], ACT.Copy).then_inc(ones_copied, 1)
                    std_of(0, 4)
                    split_hi(1, wk_hi)
                for u in range(1, UNITS):
                    tok(u)
                    v_job(u - 1)
                v_job(UNITS - 1)
                if first(o):
                    std_of(4, TILES)
                for g in range(NKV):
                    for src in range(2):
                        job = UNITS + 2 * g + src
                        act.wait_ge(projected, JOBS * o + job + 1)
                        if src == 0 and not (first(o) and g < 2):
                            act.wait_ge(k_stored[g % 2], 16 * (2 * o + g // 2))
                        act.activation(k_out[g % 2][:, :, 0, :, 64 * src:64 * src + 64],
                                       ps_a[job % 2][:].rearrange("p (q b t) -> p q b t", q=2, b=QB),
                                       ACT.Copy).then_inc(out_hi_made, 1)

            octet(0)
            with act.Fori(1, OCTETS) as o:
                octet(o)

        @block.vector
        def _(dve):
            def stats_of(lo, hi):
                for n in range(lo, hi):
                    dve.bn_stats(stats[:, n, :], y[:, n, :]).then_inc(stats_made, 1)
                for n in range(lo, hi):
                    dve.wait_ge(stats_made, n + 1)
                    dve.bn_aggr(mean_var[:, n, :], stats[:, n, :]).then_inc(meanvar_made, 1)

            def rstd_of(lo, hi, count):
                dve.wait_ge(std_made, count)
                dve.reciprocal(rstd[:, lo:hi], std[:, lo:hi]).then_inc(rstd_made, 1)

            def split_low(i, lo, hi):
                dve.wait_ge(kv_hi_made, i + 1)
                dve.tensor_tensor(lo[:], kv_raw[:, i], f32(hi[:]), ALU.subtract).then_inc(kv_lo_made, 1)

            def normalise(o, i):
                if not (first(o) and i < 2):
                    dve.wait_ge(transposed, UNITS * o + 2 * i - 2)
                n = 4 * o + i
                n = slice(n, n + 1) if first(o) else bass.ds(n, 1)
                dve.tensor_scalar(normed[i % 2][:], y[:, n, :].squeeze(1), mean_var[:, n, 0],
                                  rstd[:, n], ALU.subtract, ALU.mult).then_inc(normed_made, 1)

            def octet(o):
                def tok_low(u):
                    src, i = u % 2, u // 2
                    dve.wait_ge(tok_hi_made, UNITS * o + u + 1)
                    dve.tensor_tensor(tok_lo[:, src, :, i * P:(i + 1) * P], ps_t[u % 2][:],
                                      f32(tok_hi[:, src, :, i * P:(i + 1) * P]),
                                      ALU.subtract).then_inc(tok_lo_made, 1)

                def v_low(u):
                    dve.wait_ge(out_hi_made, JOBS * o + u + 1)
                    dve.tensor_tensor(v_out[u % 2][:, :, 1, :], ps_a[u % 2][:].rearrange("p (g d) -> p g d", g=NKV),
                                      f32(v_out[u % 2][:, :, 0, :]), ALU.subtract).then_inc(out_lo_made, 1)

                if first(o):
                    split_low(0, wv_lo, wv_hi)
                    tok_low(0)
                    dve.wait_ge(x_in, 16)
                    stats_of(0, 4)
                    rstd_of(0, 4, 1)
                    dve.wait_ge(rstd_made, 1)
                normalise(o, 0)
                normalise(o, 1)
                if first(o):
                    split_low(1, wk_lo, wk_hi)
                else:
                    tok_low(0)
                for u in range(1, UNITS):
                    tok_low(u)
                    if u in (1, 3):
                        normalise(o, 2 + u // 2)
                    v_low(u - 1)
                    if first(o) and u < 7:
                        if u % 2:
                            dve.wait_ge(x_in, 16 * (u // 2 + 2))
                        stats_of(2 + 2 * u, 4 + 2 * u)
                v_low(UNITS - 1)
                if first(o):
                    rstd_of(4, TILES, 2)
                    dve.wait_ge(rstd_made, 2)
                for g in range(NKV):
                    for src in range(2):
                        job = UNITS + 2 * g + src
                        keys = slice(64 * src, 64 * src + 64)
                        dve.wait_ge(out_hi_made, JOBS * o + job + 1)
                        for q in range(2):
                            last = dve.tensor_tensor(
                                k_out[g % 2][:, q, 1, :, keys],
                                ps_a[job % 2][:, 256 * q:256 * q + 256].rearrange("p (b t) -> p b t", b=QB),
                                f32(k_out[g % 2][:, q, 0, :, keys]), ALU.subtract)
                        last.then_inc(out_lo_made, 1)

            octet(0)
            with dve.Fori(1, OCTETS) as o:
                octet(o)

        @block.tensor
        def _(pe):
            pe.wait_ge(consts_made, 4)

            def octet(o):

                def transposes(u):
                    src, i = u % 2, u // 2
                    if u == 0:
                        pe.wait_ge(ctx_in, 16 * (o + 1))
                    if src == 1:
                        pe.wait_ge(normed_made, 4 * o + i + 1)
                    if not (first(o) and u < 2):
                        pe.wait_ge(tok_lo_made, UNITS * o + u - 1)
                    tile = normed[i % 2] if src else ctx_raw[:, i, :]
                    for c in range(C):
                        last = pe.transpose(ps_t[u % 2][:, c, :], tile[:, c * P:(c + 1) * P], ident[:])
                    last.then_inc(transposed, 1)

                def free_ps_a(job):
                    if not (first(o) and job < 2):
                        pe.wait_ge(out_lo_made, JOBS * o + job - 1)

                def v_job(u):
                    src, i = u % 2, u // 2
                    if first(o) and u == 0:
                        pe.wait_ge(kv_lo_made, 1)
                    pe.wait_ge(tok_lo_made, UNITS * o + u + 1)
                    free_ps_a(u)
                    for c in range(C):
                        t = slice(i * P, (i + 1) * P)
                        last = three_pass(pe, ps_a[u % 2][:], tok_hi[:, src, c, t], tok_lo[:, src, c, t],
                                          wv_hi[:, c, :], wv_lo[:, c, :], c == 0, c == C - 1)
                    last.then_inc(projected, 1)

                transposes(0)
                if first(o):
                    v_job(0)
                for u in range(1, UNITS):
                    transposes(u)
                    if not (first(o) and u == 1):
                        v_job(u - 1)
                v_job(UNITS - 1)
                if first(o):
                    pe.wait_ge(kv_lo_made, 2)
                for g in range(NKV):
                    for src in range(2):
                        job = UNITS + 2 * g + src
                        free_ps_a(job)
                        for c in range(C):
                            n = slice(g * DH, (g + 1) * DH)
                            last = three_pass(pe, ps_a[job % 2][:], wk_hi[:, c, n], wk_lo[:, c, n],
                                              tok_hi[:, src, c, :], tok_lo[:, src, c, :], c == 0, c == C - 1)
                        last.then_inc(projected, 1)

            octet(0)
            with pe.Fori(1, OCTETS) as o:
                octet(o)



def over_octets(eng, octet):
    octet(0, 0, 0)
    with eng.Fori(1, 3) as t:
        octet(t, t, 0)
    with eng.Fori(1, NKV) as g:
        octet(4 * g - 1, 3, g)
        octet(4 * g, 0, g)
        with eng.Fori(1, 3) as o:
            octet(4 * g + o, o, g)
    octet(15, 3, NKV)


STEPS = NKV * BATCH


class Step:

    def __init__(self, t, j):
        self.t, self.j = t, j
        self.m = 8 * t + j
        plain = isinstance(t, int)
        self.pv = not plain or 2 <= self.m < STEPS + 2
        self.exp = not plain or 1 <= self.m < STEPS + 1
        self.scores = not plain or self.m < STEPS
        self.quad = 2 * t + 1 + j // 4
        self.query = not plain or self.quad < STEPS // 4
        self.out = not plain or 4 <= self.m < STEPS + 4
        self.pair = 4 * t - 2 + j // 2
        self.add = j % 2 == 0 and (not plain or self.m >= 6)
        self.pair_parity = (j // 2) % 2

    def at_least(self, m):
        return not isinstance(self.t, int) or self.m >= m


def stage_two(nc, a, common, scratch):
    y, ones_r, gain = common["y"], common["ones_r"], common["gain_attn"]
    with ExitStack() as stack:
        b = Buffers(nc, stack)
        wq_hi = b.sb("wq_hi", [P, C, HG * DH], F32R)
        wq_lo = b.sb("wq_lo", [P, C, HG * DH], F32R)
        wo_hi = b.sb("wo_hi", [P, HG, D], F32R)
        wo_lo = b.sb("wo_lo", [P, HG, D], F32R)
        w_raw = [b.sb(f"w_raw{i}", [P, 1024]) for i in range(2)]
        xt = [b.sb(f"xt{i}", [P, 2, C, 256], F32R) for i in range(2)]
        kt = [b.sb(f"kt{i}", [P, 2, QB, KEYS], F32R) for i in range(2)]
        vt = [b.sb(f"vt{i}", [KEYS, QB, 2, DH], F32R) for i in range(2)]
        q_hi = [b.sb(f"q_hi{i}", [P, HG, 256], F32R) for i in range(2)]
        q_lo = [b.sb(f"q_lo{i}", [P, HG, 256], F32R) for i in range(2)]
        s_sb = [b.sb(f"s_sb{i}", [KEYS, 512]) for i in range(2)]
        s_max = [b.sb(f"s_max{i}", [KEYS, 512]) for i in range(2)]
        p_hi = [b.sb(f"p_hi{i}", [KEYS, 512], F32R) for i in range(2)]
        p_lo = [b.sb(f"p_lo{i}", [KEYS, 512], F32R) for i in range(2)]
        ones_col = b.sb("ones_col", [P, 1])
        zeros = b.sb("zeros", [P, 1, D])
        turn = b.sb("turn", [P, 1])
        sums = b.sb("sums", [P, 16])
        rsums = b.sb("rsums", [P, 16])
        rsum_rows = b.sb("rsum_rows", [P, 512])
        o_sb = b.sb("o_sb", [P, HG, SQ])
        o_hi = [b.sb(f"o_hi{i}", [P, HG, P], F32R) for i in range(2)]
        o_lo = [b.sb(f"o_lo{i}", [P, HG, P], F32R) for i in range(2)]
        ps_q = [b.ps(f"ps_q{i}", [P, 512]) for i in range(2)]
        ps_s = [b.ps(f"ps_s{i}", [KEYS, 512]) for i in range(2)]
        ps_sum = b.ps("ps_sum", [P, 512])
        ps_o = [b.ps(f"ps_o{i}", [P, 512]) for i in range(2)]
        ps_y = b.ps("ps_y", [P, 512])

        raw_in = [b.sem(f"raw_in{i}") for i in range(2)]
        xt_in = [b.sem(f"xt_in{i}") for i in range(2)]
        kt_in = [b.sem(f"kt_in{i}") for i in range(2)]
        vt_in = [b.sem(f"vt_in{i}") for i in range(2)]
        col_made = b.sem("col_made")
        cleared = b.sem("cleared")
        w_hi_made = b.sem("w_hi_made")
        w_lo_made = b.sem("w_lo_made")
        queries = b.sem("queries")
        q_hi_made = b.sem("q_hi_made")
        q_lo_made = b.sem("q_lo_made")
        scored = b.sem("scored")
        scores_copied = b.sem("scores_copied")
        max_made = b.sem("max_made")
        shifted = b.sem("shifted")
        exp_made = b.sem("exp_made")
        p_lo_made = b.sem("p_lo_made")
        summed = b.sem("summed")
        sums_read = b.sem("sums_read")
        rsums_made = b.sem("rsums_made")
        rsum_rows_made = b.sem("rsum_rows_made")
        weighted = b.sem("weighted")
        o_made = b.sem("o_made")
        o_hi_made = b.sem("o_hi_made")
        o_lo_made = b.sem("o_lo_made")
        halves = b.sem("halves")
        added = b.sem("added")

        wq_v = a["L0_xattn_Wq"].rearrange("(c p) (g n) -> g p c n", p=P, g=NKV)
        wo_v = a["L0_xattn_Wo"].rearrange("(g h d) n -> g d h n", g=NKV, h=HG)
        PIECES = 8

        def piece_raw(i):
            shape = dict(c=C) if i < 4 else dict(c=2)
            return w_raw[i % 2][:].rearrange("p (c n) -> p c n", **shape)

        def piece_of(w_q, w_o, i):
            return w_q[:, :, 256 * i:256 * i + 256] if i < 4 else w_o[:, 2 * i - 8:2 * i - 6, :]

        def splits_at(t, o, j):
            if isinstance(t, int):
                return [4 + j] if t == 0 and j < 4 else []
            if isinstance(o, int) and o == 3 and 1 <= j <= 4:
                return [j - 1]
            if isinstance(o, int) and o == 0 and j in (3, 4):
                return [4, 5] if j == 3 else [6, 7]
            return []

        PER_OCTET = scratch["slots_x"].shape[0] // (STEPS // 8 * P)
        slots_v = scratch["slots_x"].rearrange("(t i p) d -> t p i d", i=PER_OCTET, p=P)

        block = stack.enter_context(nc.Block())

        @block.sync
        def _(sp):
            def load_piece(g, i):
                if not (first(g) and i < 2):
                    sp.wait_ge(w_lo_made, PIECES * g + i - 1)
                src = wq_v[g, :, :, 256 * i:256 * i + 256] if i < 4 else wo_v[g, :, 2 * i - 8:2 * i - 6, :]
                sp.dma_start(piece_raw(i), src).then_inc(raw_in[i % 2], 16)

            def load_xt(quad_in_head, parity):
                sp.dma_start(f32(xt[parity][:]), scratch["x"][quad_in_head]).then_inc(xt_in[parity], 16)

            def load_kt(g, quad_in_head, parity):
                sp.dma_start(f32(kt[parity][:]).rearrange("p h b k -> p (h b k)"),
                             scratch["k"][g, quad_in_head]).then_inc(kt_in[parity], 16)

            def load_vt(g, quad_in_head, parity):
                sp.dma_start(f32(vt[parity][:]), scratch["v"][g, quad_in_head]).then_inc(vt_in[parity], 16)

            for i in range(PIECES):
                load_piece(0, i)
                if i == 0:
                    load_xt(0, 0)
                if i == 3:
                    load_kt(0, 0, 0)
                    load_xt(1, 1)
                    load_vt(0, 0, 0)

            def octet(t, o, g):
                for half in range(2):
                    q = 2 * t + half
                    if isinstance(t, int) and q == QUADS * NKV - 1:
                        break
                    wraps = isinstance(o, int) and o == 3 and half == 1
                    next_quad = 0 if wraps else 2 * o + half + 1
                    head = g - 1 if isinstance(o, int) and o == 3 and not wraps else g
                    after = (2 * o + half + 2) % 8 if isinstance(o, int) else 2 * o + half + 2
                    if not (isinstance(t, int) and q + 2 >= QUADS * NKV):
                        sp.wait_ge(queries, 4 * q + 4)
                        load_xt(after, half)
                    if not first(q):
                        sp.wait_ge(scored, 4 * q)
                    load_kt(head, next_quad, 1 - half)
                    if not first(q):
                        sp.wait_ge(weighted, 4 * q)
                    load_vt(head, next_quad, 1 - half)
                    if half == 0 and isinstance(o, int) and o == 3 and not isinstance(t, int):
                        for i in range(4):
                            load_piece(g, i)
                    if half == 1 and isinstance(o, int) and o == 3 and not isinstance(t, int):
                        load_piece(g, 4)
                        load_piece(g, 5)
                    if half == 0 and isinstance(o, int) and o == 0 and not isinstance(t, int):
                        load_piece(g, 6)
                        load_piece(g, 7)
                if first(t):
                    sp.wait_ge(col_made, 2)
                sp.dma_start(slots_v[t], zeros[:].to_broadcast([P, PER_OCTET, D])).then_inc(cleared, 16)

            over_octets(sp, octet)
            sp.wait_ge(cleared, 16 * STEPS // 8)

        @block.gpsimd
        def _(pool):
            def step(m, parity):
                pool.wait_ge(scores_copied, m + 1)
                if not (isinstance(m, int) and m < 2):
                    pool.wait_ge(shifted, m - 1)
                    pool.tensor_tensor(turn[:], ones_col[:], ones_col[:], ALU.add)
                pool.partition_all_reduce(s_max[parity][:], s_sb[parity][:], KEYS,
                                          bass.bass_isa.ReduceOp.max).then_inc(max_made, 1)

            pool.memset(ones_col[:], 1.0).then_inc(col_made, 1)
            pool.memset(zeros[:], 0.0).then_inc(col_made, 1)
            pool.wait_ge(col_made, 2)
            step(0, 0)
            step(1, 1)
            with pool.Fori(1, STEPS // 2) as i:
                step(2 * i, 0)
                step(2 * i + 1, 1)

        @block.scalar
        def _(act):
            def split_piece(g, i):
                act.wait_ge(raw_in[i % 2], 16 * (4 * g + i // 2 + 1))
                if not first(g):
                    if i < 4:
                        act.wait_ge(queries, 32 * g - 4 + i + 1)
                    else:
                        act.wait_ge(halves, 32 * g - 1 + (i - 4) // 2)
                act.activation(piece_of(wq_hi, wo_hi, i), piece_raw(i), ACT.Copy).then_inc(w_hi_made, 1)

            def query_hi(quad, quad_parity, p):
                act.wait_ge(queries, 4 * quad + p + 1)
                if p == 0 and not (isinstance(quad, int) and quad < 2):
                    act.wait_ge(scored, 4 * quad - 4)
                act.activation(q_hi[quad_parity][:, 2 * p:2 * p + 2, :],
                               ps_q[p % 2][:].rearrange("p (h t) -> p h t", h=2),
                               ACT.Copy).then_inc(q_hi_made, 1)

            def step(s, o, g):
                m, j = s.m, s.j
                if s.exp:
                    r = (j + 1) % 2
                    act.wait_ge(shifted, m)
                    if s.at_least(3):
                        act.wait_ge(weighted, m - 2)
                    act.activation(p_hi[r][:], s_sb[r][:], ACT.Exp, scale=SCALE)
                    act.activation(s_sb[r][:], s_sb[r][:], ACT.Exp, scale=SCALE).then_inc(exp_made, 1)
                if s.scores:
                    act.wait_ge(scored, m + 1)
                    if s.at_least(2):
                        act.wait_ge(p_lo_made, m - 1)
                    act.activation(s_sb[j % 2][:], ps_s[j % 2][:], ACT.Copy).then_inc(scores_copied, 1)
                if s.pv:
                    act.wait_ge(o_made, m - 1)
                    if j % 2 == 0 and s.at_least(6):
                        act.wait_ge(halves, m - 4)
                    token = slice(64 * (j % 2), 64 * (j % 2) + 64)
                    act.activation(o_hi[1 - s.pair_parity][:, :, token], o_sb[:],
                                   ACT.Copy).then_inc(o_hi_made, 1)
                if s.query:
                    query_hi(s.quad, (1 + j // 4) % 2, j % 4)
                for i in splits_at(s.t, o, j):
                    split_piece(g, i)

            split_piece(0, 0)
            for i in range(4):
                if i < 3:
                    split_piece(0, i + 1)
                query_hi(0, 0, i)
            over_octets(act, lambda t, o, g: [step(Step(t, j), o, g) for j in range(8)])
            for j in range(4):
                step(Step(16, j), 0, NKV)

        @block.vector
        def _(dve):
            def split_piece(g, i):
                dve.wait_ge(w_hi_made, PIECES * g + i + 1)
                dve.tensor_tensor(piece_of(wq_lo, wo_lo, i), piece_raw(i), f32(piece_of(wq_hi, wo_hi, i)),
                                  ALU.subtract).then_inc(w_lo_made, 1)

            def query_lo(quad, quad_parity, p):
                dve.wait_ge(q_hi_made, 4 * quad + p + 1)
                dve.tensor_tensor(q_lo[quad_parity][:, 2 * p:2 * p + 2, :],
                                  ps_q[p % 2][:].rearrange("p (h t) -> p h t", h=2),
                                  f32(q_hi[quad_parity][:, 2 * p:2 * p + 2, :]),
                                  ALU.subtract).then_inc(q_lo_made, 1)

            def add_pair(s, tile):
                dve.wait_ge(halves, s.m - 4)
                dve.scalar_tensor_tensor(out=y[:, tile, :], in0=ps_y[:], scalar=gain[:], in1=y[:, tile, :],
                                         op0=ALU.mult, op1=ALU.add).then_inc(added, 1)

            def step(s, o, g):
                m, j = s.m, s.j
                if s.add:
                    tile = 4 * o - 3 + j // 2
                    add_pair(s, tile % TILES if isinstance(tile, int) else tile)
                if s.exp:
                    r = (j + 1) % 2
                    dve.wait_ge(max_made, m)
                    dve.tensor_tensor(s_sb[r][:], s_sb[r][:], s_max[r][:], ALU.subtract).then_inc(shifted, 1)
                if s.pv:
                    dve.wait_ge(summed, m - 1)
                    dve.tensor_reduce(sums[:], ps_sum[:].rearrange("p (k c) -> p k c", c=32), AX.X, ALU.max,
                                      apply_transpose=True).then_inc(sums_read, 1)
                    dve.wait_ge(sums_read, m - 1)
                    dve.reciprocal(rsums[:], sums[:]).then_inc(rsums_made, 1)
                    dve.wait_ge(rsums_made, m - 1)
                    dve.transpose(rsum_rows[:], rsums[:].unsqueeze(2).to_broadcast([P, 16, 32])
                                  ).then_inc(rsum_rows_made, 1)
                if s.exp:
                    dve.wait_ge(exp_made, m)
                    dve.tensor_tensor(p_lo[r][:], s_sb[r][:], f32(p_hi[r][:]), ALU.subtract).then_inc(p_lo_made, 1)
                if s.pv:
                    dve.wait_ge(rsum_rows_made, m - 1)
                    dve.wait_ge(weighted, m - 1)
                    dve.tensor_tensor(o_sb[:].rearrange("p h t -> p (h t)"), ps_o[j % 2][:], rsum_rows[:],
                                      ALU.mult).then_inc(o_made, 1)
                    dve.wait_ge(o_hi_made, m - 1)
                    token = slice(64 * (j % 2), 64 * (j % 2) + 64)
                    dve.tensor_tensor(o_lo[1 - s.pair_parity][:, :, token], o_sb[:],
                                      f32(o_hi[1 - s.pair_parity][:, :, token]), ALU.subtract).then_inc(o_lo_made, 1)
                if s.query:
                    query_lo(s.quad, (1 + j // 4) % 2, j % 4)
                for i in splits_at(s.t, o, j):
                    split_piece(g, i)

            split_piece(0, 0)
            for i in range(4):
                if i < 3:
                    split_piece(0, i + 1)
                query_lo(0, 0, i)
            over_octets(dve, lambda t, o, g: [step(Step(t, j), o, g) for j in range(8)])
            for j in range(4):
                step(Step(16, j), 0, NKV)
            add_pair(Step(16, 4), TILES - 1)

        @block.tensor
        def _(pe):
            def project_queries(quad, quad_parity, p):
                for h in range(2):
                    for c in range(C):
                        n = slice((2 * p + h) * DH, (2 * p + h + 1) * DH)
                        last = three_pass(pe, ps_q[p % 2][:, 256 * h:256 * h + 256], wq_hi[:, c, n], wq_lo[:, c, n],
                                          xt[quad_parity][:, 0, c, :], xt[quad_parity][:, 1, c, :],
                                          c == 0, c == C - 1)
                last.then_inc(queries, 1)

            def step(s, o, g):
                t, m, j = s.t, s.m, s.j
                last_octet = isinstance(o, int) and o == 3
                if s.pv:
                    batch, r = (j + 2) % 4, j % 2
                    quad_parity = ((j + 6) // 4) % 2
                    if batch == 0:
                        pe.wait_ge(vt_in[quad_parity], 16 * (t + 1))
                    pe.wait_ge(p_lo_made, m - 1)
                    if s.at_least(3):
                        pe.wait_ge(sums_read, m - 2)
                    pe.matmul(ps_sum[:], ones_r[:], p_hi[r][:], start=True, stop=False)
                    pe.matmul(ps_sum[:], ones_r[:], p_lo[r][:], start=False, stop=True).then_inc(summed, 1)
                    if s.at_least(4):
                        pe.wait_ge(o_made, m - 3)
                    v = vt[quad_parity]
                    three_pass(pe, ps_o[r][:], v[:, batch, 0], v[:, batch, 1], p_hi[r][:], p_lo[r][:],
                               True, True).then_inc(weighted, 1)
                if s.scores:
                    batch, quad_parity = j % 4, j // 4
                    if batch == 0:
                        pe.wait_ge(kt_in[quad_parity], 16 * (t + 1))
                        pe.wait_ge(q_lo_made, 8 * t + 4 * quad_parity + 4)
                    if s.at_least(2):
                        pe.wait_ge(scores_copied, m - 1)
                    k = kt[quad_parity]
                    token = slice(64 * batch, 64 * batch + 64)
                    out = ps_s[j % 2][:].rearrange("p (h t) -> p h t", h=HG)
                    three_pass(pe, out, k[:, 0, batch], k[:, 1, batch], q_hi[quad_parity][:, :, token],
                               q_lo[quad_parity][:, :, token], True, True).then_inc(scored, 1)
                if s.query:
                    p, quad_parity = j % 4, (1 + j // 4) % 2
                    if p == 0:
                        pe.wait_ge(xt_in[quad_parity], 16 * (t + 1 + j // 4))
                    if last_octet and j >= 4:
                        pe.wait_ge(w_lo_made, PIECES * g + p + 1)
                    pe.wait_ge(q_lo_made, 4 * s.quad + p - 1)
                    project_queries(s.quad, quad_parity, p)
                if s.out:
                    half = j % 2
                    if half == 0:
                        pe.wait_ge(o_lo_made, m - 2)
                        if s.at_least(6):
                            pe.wait_ge(added, s.pair)
                    if isinstance(o, int) and o == 0 and j in (4, 5) and not (isinstance(t, int) and t == 16):
                        pe.wait_ge(w_lo_made, PIECES * g + 6 + 2 * half)
                    for h in range(4 * half, 4 * half + 4):
                        last = three_pass(pe, ps_y[:], o_hi[s.pair_parity][:, h, :], o_lo[s.pair_parity][:, h, :],
                                          wo_hi[:, h, :], wo_lo[:, h, :], h == 0, h == HG - 1)
                    last.then_inc(halves, 1)

            pe.wait_ge(xt_in[0], 16)
            for p in range(4):
                pe.wait_ge(w_lo_made, p + 1)
                if p >= 2:
                    pe.wait_ge(q_lo_made, p - 1)
                project_queries(0, 0, p)
            over_octets(pe, lambda t, o, g: [step(Step(t, j), o, g) for j in range(8)])
            for j in range(4):
                step(Step(16, j), 0, NKV)



SLOT = 256
SLOTS = (2 * T + E * (SLOT - 1)) // SLOT
ROOM = -(-SLOTS // 2) * 2


class SharedHalf:

    def __init__(self, b, half, ps_up, ps_down, y, moe):
        self.half, self.ps_up, self.ps_down, self.y, self.moe = half, ps_up, ps_down, y, moe
        work = b.sb(f"s_work{half}", [P, 4, 512])
        self.w_raw = work[:, 0:3]
        self.silu = [work[:, i] for i in range(2)]
        self.h_sb = [work[:, 2 + i] for i in range(2)]
        self.w_hi = b.sb(f"sw_hi{half}", [P, 3, 512], F32R)
        self.w_lo = b.sb(f"sw_lo{half}", [P, 3, 512], F32R)
        self.h_hi = [b.sb(f"s_h_hi{half}{i}", [P, 512], F32R) for i in range(2)]
        self.h_lo = [b.sb(f"s_h_lo{half}{i}", [P, 512], F32R) for i in range(2)]
        self.raw_in = b.sem(f"s_raw_in{half}")
        self.w_hi_made = b.sem(f"s_w_hi_made{half}")
        self.w_lo_made = b.sem(f"s_w_lo_made{half}")
        self.up_done = b.sem(f"s_up_done{half}")
        self.silu_made = b.sem(f"s_silu_made{half}")
        self.h_made = b.sem(f"s_h_made{half}")
        self.h_hi_made = b.sem(f"s_h_hi_made{half}")
        self.h_lo_made = b.sem(f"s_h_lo_made{half}")
        self.down_done = b.sem(f"s_down_done{half}")
        self.y_added = b.sem(f"s_y_added{half}")

    def load(self, sp, a):
        n = slice(INTER * self.half, INTER * self.half + INTER)
        for i, name in enumerate(("L0_ffn_sw1", "L0_ffn_sw2")):
            sp.dma_start(self.w_raw[:, i].rearrange("p (c n) -> p c n", c=C),
                         a[name][:, n].rearrange("(c p) n -> p c n", p=P)).then_inc(self.raw_in, 16)
        sp.dma_start(self.w_raw[:, 2], a["L0_ffn_sw3"][n, :]).then_inc(self.raw_in, 16)

    def act_split(self, act):
        act.wait_ge(self.raw_in, 48)
        act.activation(self.w_hi[:], self.w_raw, ACT.Copy).then_inc(self.w_hi_made, 1)

    def act_job(self, act, o):
        r = o % 2
        act.wait_ge(self.up_done, o + 1)
        if o >= 2:
            act.wait_ge(self.h_made, o - 1)
        act.activation(self.silu[r], self.ps_up[2 * r][:], ACT.Silu,
                       bias=self.moe["shared_bias"][:, 0, self.half:self.half + 1]).then_inc(self.silu_made, 1)
        act.wait_ge(self.h_made, o + 1)
        if o >= 2:
            act.wait_ge(self.down_done, 4 * o - 4)
        act.activation(self.h_hi[r][:], self.h_sb[r], ACT.Copy).then_inc(self.h_hi_made, 1)

    def dve_split(self, dve):
        dve.wait_ge(self.w_hi_made, 1)
        dve.tensor_tensor(self.w_lo[:], self.w_raw, f32(self.w_hi[:]), ALU.subtract).then_inc(self.w_lo_made, 1)

    def dve_h(self, dve, o):
        r = o % 2
        if o >= 2:
            dve.wait_ge(self.h_lo_made, o - 1)
        dve.wait_ge(self.silu_made, o + 1)
        dve.scalar_tensor_tensor(out=self.h_sb[r], in0=self.ps_up[2 * r + 1][:],
                                 scalar=self.moe["shared_bias"][:, 1, self.half:self.half + 1],
                                 in1=self.silu[r], op0=ALU.add, op1=ALU.mult).then_inc(self.h_made, 1)
        dve.wait_ge(self.h_hi_made, o + 1)
        dve.tensor_tensor(self.h_lo[r][:], self.h_sb[r], f32(self.h_hi[r][:]),
                          ALU.subtract).then_inc(self.h_lo_made, 1)

    def dve_add(self, dve, o, gain, combined=None):
        for i in range(4):
            dve.wait_ge(self.down_done, 4 * o + i + 1)
            n = 4 * o + i
            if combined is not None:
                dve.wait_ge(combined, 2 * n + 2)
            dve.scalar_tensor_tensor(out=self.y[:, n, :], in0=self.ps_down[i][:], scalar=gain[:],
                                     in1=self.y[:, n, :], op0=ALU.mult, op1=ALU.add).then_inc(self.y_added, 1)

    def pe_up(self, pe, o):
        r = o % 2
        if o == 0:
            pe.wait_ge(self.w_lo_made, 1)
        if o >= 2:
            pe.wait_ge(self.h_made, o - 1)
        tokens = slice(512 * o, 512 * o + 512)
        for k in range(2):
            for c in range(C):
                n = slice(INTER * c, INTER * c + INTER)
                last = three_pass(pe, self.ps_up[2 * r + k][:], self.w_hi[:, k, n], self.w_lo[:, k, n],
                                  self.moe["x_hi"][:, c, tokens], self.moe["x_lo"][:, c, tokens],
                                  c == 0, c == C - 1)
        last.then_inc(self.up_done, 1)

    def pe_down(self, pe, o):
        r = o % 2
        pe.wait_ge(self.h_lo_made, o + 1)
        for i in range(4):
            if o:
                pe.wait_ge(self.y_added, 4 * o - 4 + i + 1)
            tokens = slice(P * i, P * i + P)
            three_pass(pe, self.ps_down[i][:], self.h_hi[r][:, tokens], self.h_lo[r][:, tokens],
                       self.w_hi[:, 2], self.w_lo[:, 2], True, True).then_inc(self.down_done, 1)


def stage_three(nc, a, common, scratch, out):
    with ExitStack() as stack:
        b = Buffers(nc, stack)
        moe = {
            "x_hi": b.sb("x_hi", [P, C, T], F32R),
            "x_lo": b.sb("x_lo", [P, C, T], F32R),
            "shared_bias": b.sb("shared_bias", [P, 2, 2]),
            "slot_bias": b.sb("slot_bias", [P, 2, ROOM]),
            "slot_expert": b.sb("slot_expert", [P, ROOM], mybir.dt.int32),
            "rows": b.sb("rows", [P, 2, TILES], mybir.dt.uint32),
            "choice_gates": b.sb("choice_gates", [P, 2, TILES]),
        }
        route(nc, a, common, scratch, moe)
        experts(nc, a, common, scratch, moe, out)


def route(nc, a, common, scratch, moe):
    y, ident, gain, ones_r = common["y"], common["ident"], common["gain_ffn"], common["ones_r"]
    x_hi, x_lo = moe["x_hi"], moe["x_lo"]
    with ExitStack() as stack:
        b = Buffers(nc, stack)
        stats = b.sb("stats3", [P, TILES, 6])
        mean_var = b.sb("mean_var3", [P, TILES, 2])
        std = b.sb("std3", [P, TILES])
        rstd = b.sb("rstd3", [P, TILES])
        eps = b.sb("eps3", [P, 1])
        normed = b.sb("normed3", [P, TILES, D])
        rw_raw = b.sb("rw_raw", [P, C, E])
        rw_hi = b.sb("rw_hi", [P, C, E], F32R)
        rw_lo = b.sb("rw_lo", [P, C, E], F32R)
        rb = b.sb("rb", [E, 1])
        rbias = b.sb("rbias", [P, E])
        b3_raw = b.sb("b3_raw", [E + 1, D])
        b3_hi = b.sb("b3_hi", [E + 1, D], F32R)
        b3_lo = b.sb("b3_lo", [E + 1, D], F32R)
        bias_rows = [b.sb(f"bias_rows{i}", [E, P]) for i in range(2)]
        bias_rows_hi = [b.sb(f"bias_rows_hi{i}", [E, P], F32R) for i in range(2)]
        bias_rows_lo = [b.sb(f"bias_rows_lo{i}", [E, P], F32R) for i in range(2)]
        shared_rows = b.sb("shared_rows", [4, P])
        logits_t = b.sb("logits_t", [E, 2, 512])
        logits = b.sb("logits", [P, TILES, E])
        probs = b.sb("probs", [P, TILES, E])
        scores = b.sb("scores", [P, TILES, E])
        masked = b.sb("masked", [P, TILES, E])
        marks = b.sb("marks", [P, TILES, E])
        chosen = [b.sb(f"chosen{i}", [P, TILES, E]) for i in range(2)]
        mask = b.sb("mask", [P, TILES, E], F32R)
        gates = b.sb("gates3", [P, TILES, E + 1])
        gates_hi = [b.sb(f"gates_hi{i}", [E + 1, 512], F32R) for i in range(2)]
        gates_lo = [b.sb(f"gates_lo{i}", [E + 1, 512], F32R) for i in range(2)]
        before = b.sb("before", [P, E, E])
        thresholds = b.sb("thresholds", [P, T // SLOT])
        slot_numbers = b.sb("slot_numbers", [P, ROOM])
        partition = b.sb("partition", [P, 1])
        earlier = b.sb("earlier", [P, P])
        earlier_r = b.sb("earlier_r", [P, P], F32R)
        tile_prefix = b.sb("tile_prefix", [P, TILES, E])
        counts = b.sb("counts", [P, E])
        full = b.sb("full", [P, E, T // SLOT])
        slots_of = b.sb("slots_of", [P, E])
        pairs = b.sb("pairs", [P, E, E])
        first_slot = b.sb("first_slot", [P, E])
        last_slot = b.sb("last_slot", [P, E])
        first_row = b.sb("first_row", [P, E])
        ends = b.sb("ends", [P, ROOM, E])
        slot_expert_f = b.sb("slot_expert_f", [P, ROOM])
        slot_hot = b.sb("slot_hot", [E, ROOM], F32R)
        places = b.sb("places", [P, TILES, E])
        place = b.sb("place", [P, 2, TILES])
        row = b.sb("row", [P, TILES])
        group_max = b.sb("group_max", [P, TILES, GROUPS])
        rank = b.sb("rank", [P, TILES, GROUPS])
        beats = b.sb("beats", [P, TILES])
        order = b.sb("order", [P, E])
        banks = [b.ps(f"bank{i}", [P, 512]) for i in range(8)]
        ps_t = [bank[:].rearrange("p (c t) -> p c t", c=C) for bank in banks[0:2]]
        ps_l = banks[2][0:E, :]
        ps_turn = banks[3]
        ps_rank = banks[4]
        ps_bias = banks[5]
        ps_b3 = banks[4:6]
        ps_g = banks[6:8]
        shared = SharedHalf(b, 0, banks[0:4], banks[4:8], y, moe)

        small_in = b.sem("small_in")
        consts_made = b.sem("consts3_made")
        stats_made = b.sem("stats3_made")
        meanvar_made = b.sem("meanvar3_made")
        std_made = b.sem("std3_made")
        rstd_made = b.sem("rstd3_made")
        normed_made = b.sem("normed3_made")
        transposed = b.sem("transposed3")
        x_hi_made = b.sem("x_hi_made")
        x_lo_made = b.sem("x_lo_made")
        small_hi_made = b.sem("small_hi_made")
        small_lo_made = b.sem("small_lo_made")
        logits_t_done = b.sem("logits_t_done")
        logits_t_copied = b.sem("logits_t_copied")
        logits_turned = b.sem("logits_turned")
        bias_turned = b.sem("bias_turned")
        bias_copied = b.sem("bias_copied")
        routed = b.sem("routed")
        logits_shifted = b.sem("logits_shifted")
        exp_made = b.sem("exp3_made")
        mask_made = b.sem("mask_made")
        ranked = b.sem("ranked")
        rows_made = b.sem("rows_made")
        hot_made = b.sem("hot_made")
        slot_bias_done = b.sem("slot_bias_done")
        scattered = b.sem("scattered")
        gates_made = b.sem("gates_made")
        gates_turned = b.sem("gates_turned")
        gates_hi_made = b.sem("gates_hi_made")
        gates_lo_made = b.sem("gates_lo_made")
        b3_done = b.sem("b3_done")
        b3_added = b.sem("b3_added")

        line = lambda name: a[name].rearrange("(a b) -> a b", a=1)
        small = [(rw_raw[:], a["L0_ffn_router_w"].rearrange("(c p) e -> p c e", p=P)),
                 (rb[:], a["L0_ffn_router_b"].rearrange("(e a) -> e a", a=1)),
                 (rbias[:], line("L0_ffn_router_bias").to_broadcast([P, E])),
                 (b3_raw[0:E], a["L0_ffn_eb3"]),
                 (b3_raw[E:E + 1], line("L0_ffn_sb3")),
                 (shared_rows[0:2], a["L0_ffn_sb1"].rearrange("(s n) -> s n", s=2)),
                 (shared_rows[2:4], a["L0_ffn_sb2"].rearrange("(s n) -> s n", s=2)),
                 (bias_rows[0][:], a["L0_ffn_eb1"]),
                 (bias_rows[1][:], a["L0_ffn_eb2"])]
        SMALL = 16 * len(small)
        splits = [(rw_hi, rw_lo, rw_raw), (b3_hi, b3_lo, b3_raw)]
        splits += [(bias_rows_hi[i], bias_rows_lo[i], bias_rows[i]) for i in range(2)]

        block = stack.enter_context(nc.Block())

        @block.sync
        def _(sp):
            for dst, src in small:
                sp.dma_start(dst, src).then_inc(small_in, 16)
            shared.load(sp, a)

        @block.gpsimd
        def _(pool):
            def iota(dst, step, base=0, per_partition=0):
                pool.iota(dst, pattern=[[step, dst.shape[1]]], base=base, channel_multiplier=per_partition,
                          allow_small_or_imprecise_dtypes=True).then_inc(consts_made, 1)

            pool.memset(eps[:], EPS).then_inc(consts_made, 1)
            iota(order[:], -1, base=E)
            iota(thresholds[:], SLOT)
            iota(slot_numbers[:], 1)
            iota(partition[:], 1, per_partition=1)
            pool.memset(earlier[:], 1.0).then_inc(consts_made, 1)
            pool.memset(before[:], 1.0).then_inc(consts_made, 1)
            pool.wait_ge(consts_made, 7)
            pool.affine_select(out=earlier[:], in_=earlier[:], compare_op=ALU.is_gt, fill=0.0, base=0,
                               pattern=[[1, P]], channel_multiplier=-1).then_inc(consts_made, 1)
            pool.affine_select(out=before[:], in_=before[:], compare_op=ALU.is_gt, fill=0.0, base=0,
                               pattern=[[1, E], [-1, E]], channel_multiplier=0).then_inc(consts_made, 1)
            pool.wait_ge(rows_made, 1)
            for n in range(TILES):
                for i in range(2):
                    pool.indirect_dma_start(
                        out=scratch["slots_x"],
                        out_offset=bass.IndirectOffsetOnAxis(ap=moe["rows"][:, i, n:n + 1], axis=0),
                        in_=normed[:, n, :], in_offset=None).then_inc(scattered, 16)
            pool.wait_ge(scattered, 16 * 2 * TILES)

        @block.scalar
        def _(act):
            act.wait_ge(small_in, SMALL)
            for hi, _, raw in splits:
                act.activation(hi[:], raw[:], ACT.Copy).then_inc(small_hi_made, 1)
            act.wait_ge(consts_made, 9)
            act.activation(earlier_r[:], earlier[:], ACT.Copy).then_inc(small_hi_made, 1)

            def x_high(n):
                act.wait_ge(transposed, n + 1)
                act.activation(x_hi[:, :, n * P:(n + 1) * P], ps_t[n % 2], ACT.Copy).then_inc(x_hi_made, 1)

            def std_of(o):
                act.wait_ge(meanvar_made, 4 * o + 4)
                tiles = slice(4 * o, 4 * o + 4)
                act.activation(std[:, tiles], mean_var[:, tiles, 1], ACT.Sqrt, bias=eps[:]).then_inc(std_made, 1)

            def copy_logits(o):
                act.wait_ge(logits_t_done, o + 1)
                if o >= 2:
                    act.wait_ge(logits_turned, o - 1)
                act.activation(logits_t[:, o % 2], ps_l, ACT.Identity, bias=rb[:]).then_inc(logits_t_copied, 1)

            std_of(0)
            std_of(1)
            for n in range(TILES):
                x_high(n)
                if n == 2:
                    shared.act_split(act)
                if n % 4 == 1 and n > 4:
                    copy_logits(n // 4 - 1)
                if n % 4 == 0 and 2 <= n // 4 + 1 < OCTETS:
                    std_of(n // 4 + 1)
            copy_logits(OCTETS - 1)
            act.wait_ge(logits_shifted, 1)
            act.activation(probs[:], marks[:], ACT.Exp).then_inc(exp_made, 1)
            shared.act_job(act, 0)
            for i in range(4):
                act.wait_ge(gates_turned, i + 1)
                if i >= 2:
                    act.wait_ge(b3_done, 4 * (i - 1))
                act.activation(gates_hi[i % 2][:], ps_g[i % 2][0:E + 1, :], ACT.Copy).then_inc(gates_hi_made, 1)
            for o in range(1, OCTETS):
                shared.act_job(act, o)

        @block.vector
        def _(dve):
            def stats_of(lo, hi):
                for n in range(lo, hi):
                    dve.bn_stats(stats[:, n, :], y[:, n, :]).then_inc(stats_made, 1)
                for n in range(lo, hi):
                    dve.wait_ge(stats_made, n + 1)
                    dve.bn_aggr(mean_var[:, n, :], stats[:, n, :]).then_inc(meanvar_made, 1)

            def normalise(n):
                dve.tensor_scalar(normed[:, n, :], y[:, n, :], mean_var[:, n, 0:1], rstd[:, n:n + 1],
                                  ALU.subtract, ALU.mult).then_inc(normed_made, 1)

            def x_low(n):
                dve.wait_ge(x_hi_made, n + 1)
                tokens = slice(n * P, (n + 1) * P)
                dve.tensor_tensor(x_lo[:, :, tokens], ps_t[n % 2], f32(x_hi[:, :, tokens]),
                                  ALU.subtract).then_inc(x_lo_made, 1)

            stats_of(0, 4)
            dve.wait_ge(bias_turned, 1)
            dve.tensor_copy(moe["shared_bias"][:].rearrange("p i s -> p (i s)"),
                            ps_bias[:, 0:4]).then_inc(bias_copied, 1)
            for i, (hi, lo, raw) in enumerate(splits):
                dve.wait_ge(small_hi_made, i + 1)
                dve.tensor_tensor(lo[:], raw[:], f32(hi[:]), ALU.subtract).then_inc(small_lo_made, 1)
            def rstd_of(o):
                tiles = slice(4 * o, 4 * o + 4)
                dve.wait_ge(std_made, o + 1)
                dve.reciprocal(rstd[:, tiles], std[:, tiles]).then_inc(rstd_made, 1)
                dve.wait_ge(rstd_made, o + 1)

            rstd_of(0)
            normalise(0)
            normalise(1)
            stats_of(4, 8)
            for n in range(TILES):
                if n % 4 == 1 and n // 4 + 1 < OCTETS:
                    rstd_of(n // 4 + 1)
                if n + 2 < TILES:
                    normalise(n + 2)
                x_low(n)
                if n == 12:
                    shared.dve_split(dve)
                if n // 4 + 2 < OCTETS:
                    stats_of(n + 8, n + 9)

            count = [0]

            def link(ins):
                count[0] += 1
                ins.then_inc(routed, 1)
                dve.wait_ge(routed, count[0])

            def spread(v, width):
                return v.unsqueeze(2).to_broadcast([P, v.shape[1], width])

            def along(v, steps=TILES):
                return v.unsqueeze(1).to_broadcast([P, steps, v.shape[1]])

            def by_group(v):
                return v[:].rearrange("p n (g k) -> p (n g) k", g=GROUPS)

            def group_spread(v):
                return v[:].rearrange("p n g -> p (n g)").unsqueeze(2).to_broadcast([P, TILES * GROUPS, E // GROUPS])

            def take_best(i):
                link(dve.tensor_reduce(row[:], masked[:], AX.X, ALU.max))
                link(dve.tensor_tensor(marks[:], masked[:], spread(row[:], E), ALU.is_equal))
                link(dve.tensor_tensor(marks[:], marks[:], along(order[:]), ALU.mult))
                link(dve.tensor_reduce(row[:], marks[:], AX.X, ALU.max))
                link(dve.tensor_tensor(chosen[i][:], marks[:], spread(row[:], E), ALU.is_equal))

            dve.wait_ge(logits_turned, OCTETS)
            link(dve.tensor_copy(logits[:].rearrange("p n e -> p (n e)"), ps_turn[:, 0:TILES * E]))
            link(dve.tensor_reduce(row[:], logits[:], AX.X, ALU.max))
            dve.tensor_tensor(marks[:], logits[:], spread(row[:], E), ALU.subtract).then_inc(logits_shifted, 1)
            for g in range(GROUPS):
                link(dve.memset(rank[:, :, g], float(GROUPS - 1 - g)))
            dve.wait_ge(exp_made, 1)
            link(dve.tensor_reduce(row[:], probs[:], AX.X, ALU.add))
            link(dve.reciprocal(row[:], row[:]))
            link(dve.tensor_tensor(probs[:], probs[:], spread(row[:], E), ALU.mult))
            link(dve.tensor_tensor(scores[:], probs[:], along(rbias[:]), ALU.add))
            link(dve.tensor_reduce(group_max[:].rearrange("p n g -> p (n g)"), by_group(scores), AX.X, ALU.max))
            for g in range(GROUPS):
                for later in range(g + 1, GROUPS):
                    link(dve.tensor_tensor(beats[:], group_max[:, :, g], group_max[:, :, later], ALU.is_ge))
                    dve.tensor_tensor(rank[:, :, g], rank[:, :, g], beats[:], ALU.subtract)
                    link(dve.tensor_tensor(rank[:, :, later], rank[:, :, later], beats[:], ALU.add))
            link(dve.tensor_scalar(rank[:], rank[:], 2.0, None, ALU.is_lt))
            link(dve.tensor_tensor(by_group(masked), by_group(scores), group_spread(rank), ALU.mult))
            link(dve.tensor_scalar(rank[:], rank[:], 1.0, -LOWEST, ALU.subtract, ALU.mult))
            link(dve.tensor_tensor(by_group(masked), by_group(masked), group_spread(rank), ALU.add))
            take_best(0)
            link(dve.scalar_tensor_tensor(out=masked[:], in0=chosen[0][:], scalar=LOWEST, in1=masked[:],
                                          op0=ALU.mult, op1=ALU.add))
            take_best(1)
            dve.tensor_tensor(mask[:], chosen[0][:], chosen[1][:], ALU.add).then_inc(mask_made, 1)
            link(dve.tensor_scalar(scores[:], scores[:], gain[:], None, ALU.mult))
            for i in range(2):
                link(dve.tensor_tensor(marks[:], scores[:], chosen[i][:], ALU.mult))
                link(dve.tensor_reduce(moe["choice_gates"][:, i, :], marks[:], AX.X, ALU.add))
            dve.wait_ge(mask_made, 1)
            dve.tensor_tensor(gates[:, :, 0:E], scores[:], f32(mask[:]), ALU.mult).then_inc(gates_made, 1)
            link(dve.memset(row[:], 1.0))
            dve.tensor_scalar(gates[:, :, E:E + 1], row[:].unsqueeze(2), gain[:], None, ALU.mult).then_inc(gates_made, 1)
            shared.dve_h(dve, 0)

            dve.wait_ge(ranked, 1)
            tile_rank = ps_rank[:, 0:TILES * E].rearrange("p (n e) -> p n e", e=E)
            tile_count = ps_rank[:, TILES * E:2 * TILES * E].rearrange("p (n e) -> p n e", e=E)
            link(dve.memset(tile_prefix[:, 0, :], 0.0))
            for n in range(1, TILES):
                link(dve.tensor_tensor(tile_prefix[:, n, :], tile_prefix[:, n - 1, :], tile_count[:, n - 1, :], ALU.add))
            link(dve.tensor_tensor(counts[:], tile_prefix[:, TILES - 1, :], tile_count[:, TILES - 1, :], ALU.add))
            link(dve.tensor_tensor(full[:], spread(counts[:], T // SLOT), along(thresholds[:], E), ALU.is_gt))
            link(dve.tensor_reduce(slots_of[:], full[:], AX.X, ALU.add))
            link(dve.tensor_tensor(pairs[:], along(slots_of[:], E), before[:], ALU.mult))
            link(dve.tensor_reduce(first_slot[:], pairs[:], AX.X, ALU.add))
            dve.tensor_tensor(last_slot[:], first_slot[:], slots_of[:], ALU.add)
            link(dve.tensor_scalar(first_row[:], first_slot[:], float(SLOT), None, ALU.mult))
            link(dve.tensor_tensor(places[:], tile_rank, tile_prefix[:], ALU.add))
            link(dve.tensor_tensor(places[:], places[:], along(first_row[:]), ALU.add))
            for i in range(2):
                link(dve.tensor_tensor(marks[:], places[:], chosen[i][:], ALU.mult))
                link(dve.tensor_reduce(place[:, i, :], marks[:], AX.X, ALU.add))
            dve.tensor_copy(moe["rows"][:], place[:]).then_inc(rows_made, 1)
            link(dve.tensor_tensor(ends[:], spread(slot_numbers[:], E), along(last_slot[:], ROOM), ALU.is_ge))
            link(dve.tensor_reduce(slot_expert_f[:], ends[:], AX.X, ALU.add))
            link(dve.tensor_scalar(slot_expert_f[:], slot_expert_f[:], float(E - 1), None, ALU.min))
            dve.tensor_scalar(slot_hot[:], slot_expert_f[0:E], partition[0:E], None, ALU.is_equal).then_inc(hot_made, 1)
            dve.tensor_copy(moe["slot_expert"][:], slot_expert_f[:])
            dve.wait_ge(slot_bias_done, 1)
            dve.tensor_copy(moe["slot_bias"][:].rearrange("p i s -> p (i s)"),
                            ps_bias[:, 0:2 * ROOM]).then_inc(bias_copied, 1)

            def add_b3(n):
                dve.wait_ge(b3_done, n + 1)
                dve.tensor_tensor(y[:, n, :], ps_b3[n % 2][:], y[:, n, :], ALU.add).then_inc(b3_added, 1)

            for i in range(4):
                dve.wait_ge(gates_hi_made, i + 1)
                if i >= 2:
                    dve.wait_ge(b3_done, 4 * (i - 1))
                dve.tensor_tensor(gates_lo[i % 2][:], ps_g[i % 2][0:E + 1, :], f32(gates_hi[i % 2][:]),
                                  ALU.subtract).then_inc(gates_lo_made, 1)
                if i:
                    for n in range(4 * i - 4, 4 * i):
                        add_b3(n)
            for n in range(12, 16):
                add_b3(n)
            for o in range(1, OCTETS):
                shared.dve_h(dve, o)
                shared.dve_add(dve, o - 1, gain)
            shared.dve_add(dve, OCTETS - 1, gain)

        @block.tensor
        def _(pe):
            pe.wait_ge(small_in, SMALL)
            pe.transpose(ps_bias[:, 0:4], shared_rows[:], ident[0:4, 0:4]).then_inc(bias_turned, 1)
            pe.wait_ge(small_lo_made, 1)

            def octet_logits(o):
                pe.wait_ge(x_lo_made, 4 * o + 4)
                if o:
                    pe.wait_ge(logits_t_copied, o)
                tokens = slice(512 * o, 512 * o + 512)
                for c in range(C):
                    last = three_pass(pe, ps_l, rw_hi[:, c, :], rw_lo[:, c, :], x_hi[:, c, tokens],
                                      x_lo[:, c, tokens], c == 0, c == C - 1)
                last.then_inc(logits_t_done, 1)

            def turn_logits(o):
                pe.wait_ge(logits_t_copied, o + 1)
                for n in range(4 * o, 4 * o + 4):
                    last = pe.transpose(ps_turn[:, n * E:(n + 1) * E], logits_t[:, o % 2, (n % 4) * P:(n % 4 + 1) * P],
                                        ident[0:E, 0:E])
                last.then_inc(logits_turned, 1)

            for n in range(TILES):
                pe.wait_ge(normed_made, n + 1)
                if n >= 2:
                    pe.wait_ge(x_lo_made, n - 1)
                for c in range(C):
                    last = pe.transpose(ps_t[n % 2][:, c, :], normed[:, n, c * P:(c + 1) * P], ident[:])
                last.then_inc(transposed, 1)
                if n % 4 == 1 and n > 4:
                    octet_logits(n // 4 - 1)
                if n % 4 == 3 and n > 4:
                    turn_logits(n // 4 - 1)
            octet_logits(OCTETS - 1)
            turn_logits(OCTETS - 1)
            shared.pe_up(pe, 0)
            pe.wait_ge(logits_shifted, 1)
            shared.pe_up(pe, 1)
            pe.wait_ge(mask_made, 1)
            pe.wait_ge(small_hi_made, len(splits) + 1)
            masks = mask[:].rearrange("p n e -> p (n e)")
            pe.matmul(ps_rank[:, 0:TILES * E], earlier_r[:], masks, start=True, stop=True)
            pe.matmul(ps_rank[:, TILES * E:2 * TILES * E], ones_r[:], masks, start=True, stop=True).then_inc(ranked, 1)

            def turn_gates(i):
                for n in range(4 * i, 4 * i + 4):
                    last = pe.transpose(ps_g[i % 2][0:E + 1, (n % 4) * P:(n % 4 + 1) * P], gates[:, n, :], ident[:])
                last.then_inc(gates_turned, 1)

            pe.wait_ge(gates_made, 2)
            turn_gates(0)
            turn_gates(1)
            pe.wait_ge(hot_made, 1)
            pe.wait_ge(small_lo_made, len(splits))
            pe.wait_ge(bias_copied, 1)
            for i in range(2):
                slots = ps_bias[:, ROOM * i:ROOM * i + ROOM]
                pe.matmul(slots, bias_rows_hi[i][:], slot_hot[:], start=True, stop=False)
                last = pe.matmul(slots, bias_rows_lo[i][:], slot_hot[:], start=False, stop=True)
            last.then_inc(slot_bias_done, 1)
            pe.wait_ge(bias_copied, 2)
            for i in range(4):
                pe.wait_ge(gates_lo_made, i + 1)
                for n in range(4 * i, 4 * i + 4):
                    if n >= 2:
                        pe.wait_ge(b3_added, n - 1)
                    tokens = slice(P * (n % 4), P * (n % 4) + P)
                    three_pass(pe, ps_b3[n % 2][:], gates_hi[i % 2][:, tokens], gates_lo[i % 2][:, tokens],
                               b3_hi[:], b3_lo[:], True, True).then_inc(b3_done, 1)
                if i < 2:
                    turn_gates(i + 2)
            pe.wait_ge(b3_added, TILES)
            for o in range(OCTETS):
                shared.pe_down(pe, o)
                if o + 2 < OCTETS:
                    shared.pe_up(pe, o + 2)


def experts(nc, a, common, scratch, moe, out):
    y, ident, gain = common["y"], common["ident"], common["gain_ffn"]
    with ExitStack() as stack:
        b = Buffers(nc, stack)
        w_raw = [b.sb(f"w3_raw{i}", [P, 3, 512]) for i in range(2)]
        w_hi = [b.sb(f"w3_hi{i}", [P, 3, 512], F32R) for i in range(2)]
        w_lo = [b.sb(f"w3_lo{i}", [P, 3, 512], F32R) for i in range(2)]
        biases = [b.sb(f"biases{i}", [P, 2]) for i in range(2)]
        rows_in = [b.sb(f"rows_in{i}", [P, 2, D]) for i in range(2)]
        xs_hi = [b.sb(f"xs_hi{i}", [P, C, SLOT], F32R) for i in range(2)]
        xs_lo = [b.sb(f"xs_lo{i}", [P, C, SLOT], F32R) for i in range(2)]
        silu = [b.sb(f"silu{i}", [P, SLOT]) for i in range(2)]
        h_sb = [b.sb(f"h_sb{i}", [P, SLOT]) for i in range(2)]
        h_hi = [b.sb(f"h_hi{i}", [P, SLOT], F32R) for i in range(2)]
        h_lo = [b.sb(f"h_lo{i}", [P, SLOT], F32R) for i in range(2)]
        y_out = [b.sb(f"y_out{i}", [P, 2, D]) for i in range(2)]
        banks = [b.ps(f"bank3_{i}", [P, 512]) for i in range(8)]
        ps_t = [bank[:].rearrange("p (c t) -> p c t", c=C) for bank in banks[0:2]]
        ps_up = [bank[:].rearrange("p (k t) -> p k t", k=2) for bank in banks[2:4]]
        ps_down = banks[4:8]
        shared = SharedHalf(b, 1, banks[0:4], banks[4:8], y, moe)

        x_in = [b.sem(f"slot_x_in{i}") for i in range(2)]
        w_in = [b.sem(f"slot_w_in{i}") for i in range(2)]
        turned = b.sem("slot_turned")
        xs_hi_made = b.sem("xs_hi_made")
        xs_lo_made = b.sem("xs_lo_made")
        w_up_hi_made = b.sem("w_up_hi_made")
        w_up_lo_made = b.sem("w_up_lo_made")
        w_down_hi_made = b.sem("w_down_hi_made")
        w_down_lo_made = b.sem("w_down_lo_made")
        up_done = b.sem("up_done")
        silu_made = b.sem("silu_made")
        h_made = b.sem("h_made")
        h_hi_made = b.sem("h_hi_made")
        h_lo_made = b.sem("h_lo_made")
        down_done = b.sem("down_done")
        y_out_made = b.sem("y_out_made")
        y_stored = [b.sem(f"y_stored{i}") for i in range(2)]
        row_bufs = [buf[:, i, :] for buf in y_out + rows_in + w_raw for i in range(2)]
        ROWS = len(row_bufs)
        gathered = [b.sem(f"gathered{i}") for i in range(ROWS)]
        combined = b.sem("combined")
        stored = b.sem("stored")

        slots_x = scratch["slots_x"].rearrange("(s h p) d -> s p h d", h=2, p=P)
        slots_y = scratch["slots_y"].rearrange("(s h p) d -> s p h d", h=2, p=P)
        out_v = out.rearrange("b s d -> (b s) d").rearrange("(o i p) d -> o p i d", i=2, p=P)
        LAST = SLOTS - 1

        def late(s, m):
            return not isinstance(s, int) or s >= m

        def over_slots(eng, slot):
            for s in range(4):
                slot(s, s % 2)
            with eng.Fori(2, LAST // 2 - 1) as k:
                slot(2 * k, 0)
                slot(2 * k + 1, 1)
            for s in range(LAST // 2 * 2 - 2, SLOTS):
                slot(s, s % 2)

        block = stack.enter_context(nc.Block())

        @block.sync
        def _(sp):
            def load_x(s, r):
                if late(s, 2):
                    sp.wait_ge(turned, 2 * s - 2)
                sp.dma_start(rows_in[r][:], slots_x[s]).then_inc(x_in[r], 16)

            def load_w(s, r):
                if late(s, 2):
                    sp.wait_ge(w_up_lo_made, s - 1)
                    sp.wait_ge(w_down_lo_made, s - 1)
                column = slice(s, s + 1) if isinstance(s, int) else bass.ds(s, 1)
                e = sp.value_load(moe["slot_expert"][0:1, column], min_val=0, max_val=E - 1)
                for i, name in enumerate(("L0_ffn_ew1", "L0_ffn_ew2")):
                    sp.dma_start(w_raw[r][:, i].rearrange("p (c n) -> p c n", c=C),
                                 a[name][e].rearrange("(c p) n -> p c n", p=P)).then_inc(w_in[r], 16)
                sp.dma_start(w_raw[r][:, 2], a["L0_ffn_ew3"][e]).then_inc(w_in[r], 16)

            def slot(s, r):
                load_x(s, r)
                load_w(s, r)
                if late(s, 4):
                    store(s - 4, r)

            def store(s, r):
                sp.wait_ge(y_out_made, 2 * s + 2)
                sp.dma_start(slots_y[s], y_out[r][:]).then_inc(y_stored[r], 16)

            shared.load(sp, a)
            over_slots(sp, slot)
            for s in range(SLOTS - 4, SLOTS):
                store(s, s % 2)
            for n in range(0, TILES, 2):
                sp.wait_ge(shared.y_added, n + 2)
                sp.dma_start(out_v[n // 2], y[:, n:n + 2, :]).then_inc(stored, 16)
            sp.wait_ge(stored, 16 * TILES // 2)

        @block.gpsimd
        def _(pool):
            pool.wait_ge(y_stored[0], 16 * (SLOTS - SLOTS // 2))
            pool.wait_ge(y_stored[1], 16 * (SLOTS // 2))
            for g in range(2 * TILES):
                n, i = g // 2, g % 2
                if g >= ROWS:
                    pool.wait_ge(combined, g - ROWS + 1)
                pool.indirect_dma_start(
                    out=row_bufs[g % ROWS], out_offset=None, in_=scratch["slots_y"],
                    in_offset=bass.IndirectOffsetOnAxis(ap=moe["rows"][:, i, n:n + 1], axis=0),
                ).then_inc(gathered[g % ROWS], 16)

        @block.scalar
        def _(act):
            def xs_high(s, r):
                for half in range(2):
                    act.wait_ge(turned, 2 * s + half + 1)
                    if late(s, 2):
                        act.wait_ge(up_done, s - 1)
                    act.activation(xs_hi[r][:, :, P * half:P * half + P], ps_t[half], ACT.Copy).then_inc(xs_hi_made, 1)

            def w_up_high(s, r):
                act.wait_ge(w_in[r], 24 * (s - r) + 48)
                if late(s, 2):
                    act.wait_ge(up_done, s - 1)
                act.activation(w_hi[r][:, 0:2], w_raw[r][:, 0:2], ACT.Copy).then_inc(w_up_hi_made, 1)

            def w_down_high(s, r):
                if late(s, 2):
                    act.wait_ge(down_done, 2 * s - 2)
                act.activation(w_hi[r][:, 2], w_raw[r][:, 2], ACT.Copy).then_inc(w_down_hi_made, 1)

            def evacuate(s, r):
                for half in range(2):
                    act.wait_ge(down_done, 2 * s + half + 1)
                    if late(s, 2):
                        act.wait_ge(y_stored[r], 8 * (s - r))
                    act.activation(y_out[r][:, half], ps_down[2 * r + half][:], ACT.Copy).then_inc(y_out_made, 1)

            def slot(s, r):
                if not (isinstance(s, int) and s == LAST):
                    xs_high(s + 1, 1 - r)
                    w_up_high(s + 1, 1 - r)
                act.wait_ge(up_done, s + 1)
                if late(s, 2):
                    act.wait_ge(h_made, s - 1)
                act.activation(silu[r][:], ps_up[r][:, 0], ACT.Silu, bias=biases[r][:, 0:1]).then_inc(silu_made, 1)
                act.wait_ge(h_made, s + 1)
                if late(s, 2):
                    act.wait_ge(down_done, 2 * s - 2)
                act.activation(h_hi[r][:], h_sb[r][:], ACT.Copy).then_inc(h_hi_made, 1)
                if late(s, 1):
                    evacuate(s - 1, 1 - r)
                if not (isinstance(s, int) and s == LAST):
                    w_down_high(s + 1, 1 - r)

            shared.act_split(act)
            xs_high(0, 0)
            w_up_high(0, 0)
            w_down_high(0, 0)
            over_slots(act, slot)
            evacuate(LAST, LAST % 2)
            for o in range(OCTETS):
                shared.act_job(act, o)

        @block.vector
        def _(dve):
            def xs_low(s, r):
                for half in range(2):
                    dve.wait_ge(xs_hi_made, 2 * s + half + 1)
                    part = slice(P * half, P * half + P)
                    dve.tensor_tensor(xs_lo[r][:, :, part], ps_t[half], f32(xs_hi[r][:, :, part]),
                                      ALU.subtract).then_inc(xs_lo_made, 1)

            def w_up_low(s, r):
                dve.wait_ge(w_up_hi_made, s + 1)
                dve.tensor_tensor(w_lo[r][:, 0:2], w_raw[r][:, 0:2], f32(w_hi[r][:, 0:2]), ALU.subtract)
                column = slice(s, s + 1) if isinstance(s, int) else bass.ds(s, 1)
                dve.tensor_copy(biases[r][:], moe["slot_bias"][:, :, column].rearrange("p i a -> p (i a)")
                                ).then_inc(w_up_lo_made, 1)

            def w_down_low(s, r):
                dve.wait_ge(w_down_hi_made, s + 1)
                dve.tensor_tensor(w_lo[r][:, 2], w_raw[r][:, 2], f32(w_hi[r][:, 2]), ALU.subtract
                                  ).then_inc(w_down_lo_made, 1)

            def slot(s, r):
                if not (isinstance(s, int) and s == LAST):
                    xs_low(s + 1, 1 - r)
                    w_up_low(s + 1, 1 - r)
                if late(s, 2):
                    dve.wait_ge(h_lo_made, s - 1)
                dve.wait_ge(silu_made, s + 1)
                dve.scalar_tensor_tensor(out=h_sb[r][:], in0=ps_up[r][:, 1], scalar=biases[r][:, 1:2], in1=silu[r][:],
                                         op0=ALU.add, op1=ALU.mult).then_inc(h_made, 1)
                dve.wait_ge(h_hi_made, s + 1)
                dve.tensor_tensor(h_lo[r][:], h_sb[r][:], f32(h_hi[r][:]), ALU.subtract).then_inc(h_lo_made, 1)
                if not (isinstance(s, int) and s == LAST):
                    w_down_low(s + 1, 1 - r)

            def combine(o):
                for g in range(8 * o, 8 * o + 8):
                    n, i = g // 2, g % 2
                    dve.wait_ge(gathered[g % ROWS], 16 * (g // ROWS + 1))
                    if i:
                        dve.wait_ge(combined, g)
                    dve.scalar_tensor_tensor(out=y[:, n, :], in0=row_bufs[g % ROWS],
                                             scalar=moe["choice_gates"][:, i, n:n + 1], in1=y[:, n, :],
                                             op0=ALU.mult, op1=ALU.add).then_inc(combined, 1)

            shared.dve_split(dve)
            xs_low(0, 0)
            w_up_low(0, 0)
            w_down_low(0, 0)
            over_slots(dve, slot)
            shared.dve_h(dve, 0)
            for o in range(OCTETS):
                if o + 1 < OCTETS:
                    shared.dve_h(dve, o + 1)
                combine(o)
                shared.dve_add(dve, o, gain, combined)

        @block.tensor
        def _(pe):
            def turn(s, r):
                for half in range(2):
                    if half == 0:
                        pe.wait_ge(x_in[r], 8 * (s - r) + 16)
                    if late(s, 1):
                        pe.wait_ge(xs_lo_made, 2 * s + half - 1)
                    for c in range(C):
                        last = pe.transpose(ps_t[half][:, c, :], rows_in[r][:, half, c * P:(c + 1) * P], ident[:])
                    last.then_inc(turned, 1)

            def up(s, r):
                pe.wait_ge(w_up_lo_made, s + 1)
                pe.wait_ge(xs_lo_made, 2 * s + 2)
                if late(s, 2):
                    pe.wait_ge(h_made, s - 1)
                for k in range(2):
                    for c in range(C):
                        n = slice(INTER * c, INTER * c + INTER)
                        last = three_pass(pe, ps_up[r][:, k], w_hi[r][:, k, n], w_lo[r][:, k, n],
                                          xs_hi[r][:, c, :], xs_lo[r][:, c, :], c == 0, c == C - 1)
                last.then_inc(up_done, 1)

            def down(s, r):
                pe.wait_ge(h_lo_made, s + 1)
                pe.wait_ge(w_down_lo_made, s + 1)
                for half in range(2):
                    if late(s, 2):
                        pe.wait_ge(y_out_made, 2 * s + half - 3)
                    part = slice(P * half, P * half + P)
                    three_pass(pe, ps_down[2 * r + half][:], h_hi[r][:, part], h_lo[r][:, part], w_hi[r][:, 2],
                               w_lo[r][:, 2], True, True).then_inc(down_done, 1)

            def slot(s, r):
                if not (isinstance(s, int) and s == LAST):
                    turn(s + 1, 1 - r)
                up(s, r)
                if late(s, 1):
                    down(s - 1, 1 - r)

            turn(0, 0)
            over_slots(pe, slot)
            down(LAST, LAST % 2)
            pe.wait_ge(h_made, SLOTS)
            shared.pe_up(pe, 0)
            shared.pe_up(pe, 1)
            pe.wait_ge(y_out_made, 2 * SLOTS)
            for o in range(OCTETS):
                shared.pe_down(pe, o)
                if o + 2 < OCTETS:
                    shared.pe_up(pe, o + 2)




INS = ['x', 'ctx_4096', 'g_xattn', 'g_ffn', 'L0_xattn_Wq', 'L0_xattn_Wk', 'L0_xattn_Wv', 'L0_xattn_Wo',
       'L0_ffn_router_w', 'L0_ffn_router_b', 'L0_ffn_router_bias', 'L0_ffn_ew1', 'L0_ffn_eb1',
       'L0_ffn_ew2', 'L0_ffn_eb2', 'L0_ffn_ew3', 'L0_ffn_eb3', 'L0_ffn_sw1', 'L0_ffn_sb1',
       'L0_ffn_sw2', 'L0_ffn_sb2', 'L0_ffn_sw3', 'L0_ffn_sb3']


def program(nc, a, out):
    scratch = {
        "x": nc.dram_tensor("x_scratch", (QUADS, P, 2, C, 256), F32, kind="Internal").ap(),
        "k": nc.dram_tensor("k_scratch", (NKV, QUADS, P, 2 * QB * KEYS), F32, kind="Internal").ap(),
        "v": nc.dram_tensor("v_scratch", (NKV, QUADS, KEYS, QB, 2, DH), F32, kind="Internal").ap(),
        "slots_x": nc.dram_tensor("slots_x", (ROOM * SLOT, D), F32, kind="Internal").ap(),
        "slots_y": nc.dram_tensor("slots_y", (SLOTS * SLOT, D), F32, kind="Internal").ap(),
    }
    with ExitStack() as stack:
        b = Buffers(nc, stack)
        common = {
            "y": b.sb("y", [P, TILES, D]),
            "ident": b.sb("ident", [P, P]),
            "ones_r": b.sb("ones_r", [P, P], F32R),
            "gain_attn": b.sb("gain_attn", [P, 1]),
            "gain_ffn": b.sb("gain_ffn", [P, 1]),
        }
        stage_one(nc, a, common, scratch)
        stage_two(nc, a, common, scratch)
        stage_three(nc, a, common, scratch, out)


def kernel(**inputs):
    import concourse.bacc as bacc
    from concourse.bass_utils import run_bass_kernel_spmd as run

    nc = bacc.Bacc("TRN2", target_bir_lowering=False, num_devices=1)
    arrays, args = {}, {}
    for name in INS:
        arr = np.ascontiguousarray(inputs[name])
        arrays[f"in_{name}"] = arr
        args[name] = nc.dram_tensor(f"in_{name}", arr.shape, mybir.dt.from_np(arr.dtype),
                                    kind="ExternalInput").ap()
    out = nc.dram_tensor("out_0", (BATCH, SQ, D), F32, kind="ExternalOutput").ap()
    program(nc, args, out)
    r = run(nc, [arrays], core_ids=[0])
    return r.results[0]["out_0"]
```
